# Optimizing a Trainium2 kernel written in Bass

```python
import numpy as np
import jax
import jax.numpy as jnp

def _softmax(x, axis=-1):
    return jax.nn.softmax(x, axis=axis)

def _gelu(x):
    return jax.nn.gelu(x, approximate=True)

def _silu(x):
    return jax.nn.silu(x)

def _sigmoid(x):
    return jax.nn.sigmoid(x)

def _layernorm(x, axis=-1, eps=1e-05):
    m = jnp.mean(x, axis=axis, keepdims=True)
    v = jnp.var(x, axis=axis, keepdims=True)
    return (x - m) / jnp.sqrt(v + eps)

def _scatter_add(tgt, idx, src, axis=0):
    return tgt.at[idx].add(src)

def _segment_sum(src, seg, n):
    return jax.ops.segment_sum(src, seg, n)
kernel_name = 'mk_flamingo_gated_d1_seqx_r8_5738bb'

def setup_inputs(seed: int=0):
    np.random.seed(seed)
    _w = jnp.asarray

    def _rec_inputs():
        import jax
        import jax.numpy as jnp
        _rk = jax.random.key(seed)
        x = 7.22e-05 + 1 * jax.random.normal(jax.random.fold_in(_rk, 1), (32, 128, 128), jnp.float32)
        _lenS = 128 - jax.random.randint(jax.random.fold_in(_rk, 7), (32,), 0, max(1, 128 // 4) + 1, jnp.int32)
        _lenS2 = 77 - jax.random.randint(jax.random.fold_in(_rk, 8), (32,), 0, max(1, 77 // 4) + 1, jnp.int32)
        _ctx_1024P = jax.random.normal(jax.random.fold_in(_rk, 11), (32, 16, 128), jnp.float32)
        _ctx_1024c = jax.random.dirichlet(jax.random.fold_in(_rk, 511), 0.3 * jnp.ones((16,), jnp.float32), (32, 77))
        _ctx_1024t = jnp.einsum('bsk,bkd->bsd', _ctx_1024c, _ctx_1024P)
        _ctx_1024t = _ctx_1024t * jax.lax.rsqrt(jnp.mean(jnp.square(_ctx_1024t)) + 1e-12) * 0.953939
        ctx_1024 = 4.13588e-05 + 0.999923 * (_ctx_1024t + 0.3 * jax.random.normal(jax.random.fold_in(_rk, 611), (32, 77, 128), jnp.float32))
        _g = jax.random.normal(jax.random.fold_in(_rk, 9001), (2, 1), jnp.float32)
        _g = jnp.sign(_g) * jnp.maximum(jnp.abs(_g), 1.0) + (_g == 0) * 1.0
        g_xattn = _g[0]
        g_ffn = _g[1]
        return (x, ctx_1024, g_xattn, g_ffn)
    x, ctx_1024, g_xattn, g_ffn = _rec_inputs()

    def _L0_xattn_setup():
        import jax, jax.numpy as jnp
        import numpy as np
        D_MODEL = 128
        H = 16
        D_K = D_MODEL // H
        key = jax.random.key(seed)
        ks = jax.random.split(key, 7)
        B, S = (4, 256)
        q = jax.random.normal(ks[0], (B, S, D_MODEL), dtype=jnp.float32)
        k = jax.random.normal(ks[1], (B, S, D_MODEL), dtype=jnp.float32)
        v = jax.random.normal(ks[2], (B, S, D_MODEL), dtype=jnp.float32)
        scale = 1.0 / np.sqrt(D_MODEL)
        w_q = jax.random.normal(ks[3], (D_MODEL, D_MODEL), dtype=jnp.float32) * scale
        w_k = jax.random.normal(ks[4], (D_MODEL, D_MODEL), dtype=jnp.float32) * scale
        w_v = jax.random.normal(ks[5], (D_MODEL, D_MODEL), dtype=jnp.float32) * scale
        w_o = jax.random.normal(ks[6], (D_MODEL, D_MODEL), dtype=jnp.float32) * scale
        return {'q': q, 'k': k, 'v': v, 'w_q': w_q, 'w_k': w_k, 'w_v': w_v, 'w_o': w_o}
    _L0_xattn_all = _L0_xattn_setup()
    _L0_xattn_in = {k: v for k, v in _L0_xattn_all.items() if k in ('w_q', 'w_k', 'w_v', 'w_o')}
    del _L0_xattn_all

    def _L0_ffn_setup():
        import jax, jax.numpy as jnp
        import numpy as np
        D_MODEL = 128
        D_FF = 512
        NUM_M = 2
        E_ROUTER = 8 * NUM_M - 1
        D_FF_R = D_FF // NUM_M
        TOP_K = NUM_M * 2 - 1
        B, T = (2, 256)

        def _expert_stack(x, W1, b1, W2, b2):
            h = jax.nn.gelu(jnp.einsum('btd,edf->ebtf', x, W1) + b1[:, None, None, :], approximate=False)
            return jnp.einsum('ebtf,efd->ebtd', h, W2) + b2[:, None, None, :]
        key = jax.random.key(seed)
        ks = jax.random.split(key, 12)
        s = lambda fan_in: 1.0 / np.sqrt(fan_in)
        x = jax.random.normal(ks[0], (B, T, D_MODEL), dtype=jnp.float32)
        sW1 = jax.random.uniform(ks[1], (1, D_MODEL, D_FF), jnp.float32, -s(D_MODEL), s(D_MODEL))
        sb1 = jax.random.uniform(ks[2], (1, D_FF), jnp.float32, -s(D_MODEL), s(D_MODEL))
        sW2 = jax.random.uniform(ks[3], (1, D_FF, D_MODEL), jnp.float32, -s(D_FF), s(D_FF))
        sb2 = jax.random.uniform(ks[4], (1, D_MODEL), jnp.float32, -s(D_FF), s(D_FF))
        rW1 = jax.random.uniform(ks[5], (E_ROUTER, D_MODEL, D_FF_R), jnp.float32, -s(D_MODEL), s(D_MODEL))
        rb1 = jax.random.uniform(ks[6], (E_ROUTER, D_FF_R), jnp.float32, -s(D_MODEL), s(D_MODEL))
        rW2 = jax.random.uniform(ks[7], (E_ROUTER, D_FF_R, D_MODEL), jnp.float32, -s(D_FF_R), s(D_FF_R))
        rb2 = jax.random.uniform(ks[8], (E_ROUTER, D_MODEL), jnp.float32, -s(D_FF_R), s(D_FF_R))
        gW = jax.random.uniform(ks[9], (D_MODEL, E_ROUTER), jnp.float32, -s(D_MODEL), s(D_MODEL))
        gb = jax.random.uniform(ks[10], (E_ROUTER,), jnp.float32, -s(D_MODEL), s(D_MODEL))
        return {'x': x, 'sW1': sW1, 'sb1': sb1, 'sW2': sW2, 'sb2': sb2, 'rW1': rW1, 'rb1': rb1, 'rW2': rW2, 'rb2': rb2, 'gW': gW, 'gb': gb}
    _L0_ffn_all = _L0_ffn_setup()
    _L0_ffn_in = {k: v for k, v in _L0_ffn_all.items() if k in ('sW1', 'sb1', 'sW2', 'sb2', 'rW1', 'rb1', 'rW2', 'rb2', 'gW', 'gb')}
    del _L0_ffn_all
    return {'x': x, 'ctx_1024': ctx_1024, 'g_xattn': g_xattn, 'g_ffn': g_ffn, 'L0_xattn_w_q': _L0_xattn_in['w_q'], 'L0_xattn_w_k': _L0_xattn_in['w_k'], 'L0_xattn_w_v': _L0_xattn_in['w_v'], 'L0_xattn_w_o': _L0_xattn_in['w_o'], 'L0_ffn_sW1': _L0_ffn_in['sW1'], 'L0_ffn_sb1': _L0_ffn_in['sb1'], 'L0_ffn_sW2': _L0_ffn_in['sW2'], 'L0_ffn_sb2': _L0_ffn_in['sb2'], 'L0_ffn_rW1': _L0_ffn_in['rW1'], 'L0_ffn_rb1': _L0_ffn_in['rb1'], 'L0_ffn_rW2': _L0_ffn_in['rW2'], 'L0_ffn_rb2': _L0_ffn_in['rb2'], 'L0_ffn_gW': _L0_ffn_in['gW'], 'L0_ffn_gb': _L0_ffn_in['gb']}

def reference(x, ctx_1024, g_xattn, g_ffn, L0_xattn_w_q, L0_xattn_w_k, L0_xattn_w_v, L0_xattn_w_o, L0_ffn_sW1, L0_ffn_sb1, L0_ffn_sW2, L0_ffn_sb2, L0_ffn_rW1, L0_ffn_rb1, L0_ffn_rW2, L0_ffn_rb2, L0_ffn_gW, L0_ffn_gb):
    import jax
    import jax.numpy as jnp

    def _L0_xattn_ref(q, k, v, w_q, w_k, w_v, w_o):
        import jax, jax.numpy as jnp
        import numpy as np
        D_MODEL = 128
        H = 16
        D_K = D_MODEL // H
        B, S, _ = q.shape

        def proj(x, w):
            y = jnp.einsum('bsd,ed->bse', x, w)
            return y.reshape(B, -1, H, D_K).transpose(0, 2, 1, 3)
        query = proj(q, w_q)
        key_ = proj(k, w_k)
        value = proj(v, w_v)
        scores = jnp.einsum('bhqd,bhkd->bhqk', query, key_) / jnp.sqrt(jnp.float32(D_K))
        attn = jax.nn.softmax(scores, axis=-1)
        x = jnp.einsum('bhqk,bhkd->bhqd', attn, value)
        x = x.transpose(0, 2, 1, 3).reshape(B, S, H * D_K)
        return jnp.einsum('bsd,ed->bse', x, w_o)

    def _L0_ffn_ref(x, sW1, sb1, sW2, sb2, rW1, rb1, rW2, rb2, gW, gb):
        import jax, jax.numpy as jnp
        import numpy as np
        D_MODEL = 128
        D_FF = 512
        NUM_M = 2
        E_ROUTER = 8 * NUM_M - 1
        D_FF_R = D_FF // NUM_M
        TOP_K = NUM_M * 2 - 1
        B, T = (2, 256)

        def _expert_stack(x, W1, b1, W2, b2):
            h = jax.nn.gelu(jnp.einsum('btd,edf->ebtf', x, W1) + b1[:, None, None, :], approximate=False)
            return jnp.einsum('ebtf,efd->ebtd', h, W2) + b2[:, None, None, :]
        shared_enc = _expert_stack(x, sW1, sb1, sW2, sb2).sum(0)
        weights = jax.nn.softmax(x @ gW + gb, axis=-1)
        topv, topi = jax.lax.top_k(weights, TOP_K)
        gated = (jax.nn.one_hot(topi, E_ROUTER, dtype=weights.dtype) * topv[..., None]).sum(axis=-2)
        router_out = _expert_stack(x, rW1, rb1, rW2, rb2)
        router_enc = jnp.einsum('ebtd,bte->btd', router_out, gated)
        return shared_enc + router_enc + x
    x = x + jnp.tanh(g_xattn[0]) * _L0_xattn_ref(_layernorm(x, axis=-1), ctx_1024, ctx_1024, L0_xattn_w_q, L0_xattn_w_k, L0_xattn_w_v, L0_xattn_w_o)
    x = x + jnp.tanh(g_ffn[0]) * _L0_ffn_ref(_layernorm(x, axis=-1), L0_ffn_sW1, L0_ffn_sb1, L0_ffn_sW2, L0_ffn_sb2, L0_ffn_rW1, L0_ffn_rb1, L0_ffn_rW2, L0_ffn_rb2, L0_ffn_gW, L0_ffn_gb)
    return x

_drawn_inputs = setup_inputs


def setup_inputs(seed=0):
    import zlib

    import numpy as np

    out = dict(_drawn_inputs(seed))
    spreads = {}
    factors = {'L0_ffn_rb1': 3.745}
    for name, (base, spread) in spreads.items():
        noise = np.random.default_rng([zlib.crc32(name.encode()), seed]).standard_normal(out[name].shape)
        drawn = base * np.exp(spread * noise) if base else spread * noise
        out[name] = jnp.asarray(drawn.astype(out[name].dtype))
    for name, factor in factors.items():
        out[name] = (out[name] * factor).astype(out[name].dtype)
    return out
```

```python
from contextlib import ExitStack

import concourse.bass as bass
from concourse import mybir

P = 128
F32 = mybir.dt.float32
ALU = mybir.AluOpType
ACT = mybir.ActivationFunctionType
AX = mybir.AxisListType
EPS = 1e-5


def flamingo_kernel(nc, x, ctxT, g_xattn, g_ffn, wqT, wkT, wvT, woT, w1_chunks, b1_cols, w2_chunks, sb2,
                    rb2, gW, gb, ident, head_of_row, den_sel, rev_idx, out):
    B, S, D = x.shape
    KV = ctxT.shape[1] // B
    H, DK = 16, 8
    HQ = P // DK // 4
    GB = 4
    NG = B // GB
    GT = GB * S
    E = gW.shape[1]
    NCH = w1_chunks.shape[1]
    CR, CS = 2, 4
    assert NCH == CS + E * CR
    SCALE = float(DK) ** -0.5
    BODY = 2 * GB
    LEAD = 2

    with ExitStack() as ctx:
        def sb(name, shape):
            return ctx.enter_context(nc.sbuf_tensor(name, shape, F32))

        def sem(name):
            return ctx.enter_context(nc.semaphore(name))

        x_all = sb("x_all", [P, B, D])
        ctx_buf = sb("ctx_buf", [P, 2, GB * KV])
        w_qT, w_kT, w_vT, w_oT = (sb(n, [P, P]) for n in ("w_qT", "w_kT", "w_vT", "w_oT"))
        w1 = sb("w1", [P, NCH, P])
        w2 = sb("w2", [P, NCH, P])
        b1c = sb("b1c", [P, NCH])
        b2row = sb("b2row", [E, D])
        sb2_bc = sb("sb2_bc", [P, D])
        gw_sb = sb("gw_sb", [P, E])
        gb_bc = sb("gb_bc", [P, E])
        ident_sb = sb("ident_sb", [P, P])
        head_mask = sb("head_mask", [P, HQ])
        den_lhs = sb("den_lhs", [P, HQ, 32])
        rev_sb = sb("rev_sb", [P, E])
        neg_ones = sb("neg_ones", [P, KV])
        half_pow = sb("half_pow", [P, B])
        gates = sb("gates", [P, 2])
        tanh_g = sb("tanh_g", [P, 2])
        stats = sb("stats", [P, GB, 6])
        mv1 = sb("mv1", [P, GB, 2])
        var1 = sb("var1", [P, GB])
        rstd1 = sb("rstd1", [P, GB])
        xn = sb("xn", [P, GB, D])
        xnT = sb("xnT", [P, GT])
        qT = sb("qT", [P, 2, GT])
        q_exp = sb("q_exp", [P, 2, GB, HQ, S])
        kT = sb("kT", [P, 2, GB, KV])
        k_exp = sb("k_exp", [P, 2, GB, HQ, KV])
        v_exp = sb("v_exp", [P, 2, GB, HQ * (P + DK)])
        m_exp_q = sb("m_exp_q", [P, 2, HQ * (P + 1)])
        m_exp = sb("m_exp", [P, 2, HQ * S])
        probs = sb("probs", [P, 2, H * S])
        r_den = sb("r_den", [P, S])
        onT = sb("onT", [P, S])
        stats2 = sb("stats2", [P, B, 6])
        mv2 = sb("mv2", [P, B, 2])
        var2 = sb("var2", [P, B])
        rstd2 = sb("rstd2", [P, B])
        xn2T = sb("xn2T", [P, B * S])
        xn2T_buf = sb("xn2T_buf", [P, GT])
        logits = sb("logits", [P, B, E])
        wts = sb("wts", [P, B, E])
        pick = sb("pick", [P, B, E])
        pick2 = sb("pick2", [P, B, E])
        red = sb("red", [P, B])
        gated = sb("gated", [P, B, E])
        gated_g = sb("gated_g", [P, 2, GB, E])
        gatedT = sb("gatedT", [E, GT])
        hid = q_exp[:, 0, :, :, :].rearrange("p b h s -> p (b h s)")[:, 0:2 * GT].rearrange("p (r t) -> p r t", r=2)
        acc = q_exp[:, 1, :, :, :].rearrange("p b h s -> p (b h s)")[:, 0:2 * GT].rearrange("p (r t) -> p r t", r=2)

        psum = ctx.enter_context(nc.psum_tensor("psum", [P, 8, 512], F32))
        s_ps = psum[:, 0:2, :]
        st_ps = [psum[:, 2:4, :], psum[:, 4:6, :]]
        m_ps = psum[:, 6, :]
        o_ps = psum[:, 7, 0:S]
        den_ps = psum[:, 7, S:2 * S]
        y_ps = psum[:, 7, 2 * S:3 * S]

        passed = sem("passed")
        w_in = sem("w_in")
        x_in = sem("x_in")
        moe_in = sem("moe_in")
        zeroed = sem("zeroed")
        tanh_done = sem("tanh_done")
        ln1_var = sem("ln1_var")
        ln1_rstd = sem("ln1_rstd")
        xn_ready = sem("xn_ready")
        front_done = sem("front_done")
        front_out = sem("front_out")
        k_exp_ready = sem("k_exp_ready")
        q_exp_ready = sem("q_exp_ready")
        s_done = sem("s_done")
        max_done = sem("max_done")
        mT_done = sem("mT_done")
        m_ready = sem("m_ready")
        st_done = sem("st_done")
        exp_done = sem("exp_done")
        av_done = sem("av_done")
        rden_done = sem("rden_done")
        on_ready = sem("on_ready")
        wo_done = sem("wo_done")
        x1_done = sem("x1_done")
        dve_step = sem("dve_step")

        ln2_var = sem("ln2_var")
        ln2_rstd = sem("ln2_rstd")
        xn2_ready = sem("xn2_ready")
        x2T_done = sem("x2T_done")
        x2T_out = sem("x2T_out")
        x2T_kept = sem("x2T_kept")
        lg_done = sem("lg_done")
        lg_out = sem("lg_out")
        soft_in = sem("soft_in")
        soft_exp = sem("soft_exp")
        gated_ready = sem("gated_ready")
        ln1_a = sem("ln1_a")
        ln1_b = sem("ln1_b")
        stats2_done = sem("stats2_done")
        mv2_done = sem("mv2_done")
        gates_in = sem("gates_in")
        acc_step = sem("acc_step")
        gT_done = sem("gT_done")
        gT_out = sem("gT_out")
        bias_done = sem("bias_done")
        acc_init = sem("acc_init")
        l1_done = sem("l1_done")
        gelu_done = sem("gelu_done")
        l2_done = sem("l2_done")
        acc_done = sem("acc_done")
        y_ready = sem("y_ready")
        y_out = sem("y_out")

        block = ctx.enter_context(nc.Block())

        def walk(eng, slot):
            for o in range(LEAD):
                slot(0, o)
            with eng.Fori(0, NG // 2 - 1) as i:
                for o in range(LEAD, LEAD + BODY):
                    slot(i, o)
            for o in range(LEAD, BODY + 2):
                slot(NG // 2 - 1, o)

        def below(i, o, limit):
            return not isinstance(i, int) or i * BODY + o < limit

        @block.sync
        def _(sp):
            for dst, src in ((w_qT, wqT), (w_kT, wkT), (w_vT, wvT), (w_oT, woT), (ident_sb, ident),
                             (head_mask, head_of_row), (den_lhs, den_sel)):
                sp.dma_start(dst[:], src).then_inc(w_in, 16)

            def load_group(i, u):
                g = i * 2 + u
                sp.wait_ge(x_in, g * 32)
                if not isinstance(i, int) or i > 0:
                    sp.wait_ge(front_out, i * BODY + GB * (u - 1))
                sp.dma_start(x_all[:, bass.ds(g * GB, GB), :],
                             x[bass.ds(g * GB, GB), :, :].rearrange("b t d -> t b d")).then_inc(x_in, 16)
                sp.dma_start(ctx_buf[:, u, :], ctxT[:, bass.ds(g * (GB * KV), GB * KV)]).then_inc(x_in, 16)

            for u in range(2):
                load_group(0, u)
            with sp.Fori(1, NG // 2) as i:
                for u in range(2):
                    load_group(i, u)
            with sp.Fori(0, NG // 2) as j:
                for u in range(2):
                    sp.wait_ge(y_ready, j * 2 + (u + 1))
                    sp.dma_start(out[bass.ds((j * 2 + u) * GB, GB), :, :].rearrange("b t d -> t b d"),
                                 acc[:, u, :].rearrange("p (b d) -> p b d", b=GB)).then_inc(y_out, 16)
                    sp.wait_ge(y_out, j * 32 + (u + 1) * 16)
                    sp.sem_inc(passed, 1)

        @block.gpsimd
        def _(pool):
            pool.memset(m_exp_q[:], 0.0)
            pool.memset(v_exp[:], 0.0)
            pool.memset(neg_ones[:], -1.0)
            pool.memset(half_pow[:], -0.5).then_inc(zeroed, 1)
            pool.dma_start(gates[:, 0:1], g_xattn.rearrange("(a b) -> a b", a=1).partition_broadcast(P)).then_inc(moe_in, 16)
            pool.dma_start(gates[:, 1:2], g_ffn.rearrange("(a b) -> a b", a=1).partition_broadcast(P)).then_inc(moe_in, 16)
            pool.dma_start(sb2_bc[:], sb2.partition_broadcast(P)).then_inc(moe_in, 16)
            pool.dma_start(gb_bc[:], gb.rearrange("(a e) -> a e", a=1).partition_broadcast(P)).then_inc(moe_in, 16)
            pool.dma_start(rev_sb[:], rev_idx).then_inc(moe_in, 16)
            pool.dma_start(gw_sb[:], gW).then_inc(moe_in, 16)
            pool.dma_start(b2row[:], rb2).then_inc(moe_in, 16)
            pool.dma_start(b1c[:], b1_cols).then_inc(moe_in, 16)
            pool.dma_start(w1[:], w1_chunks).then_inc(moe_in, 16)
            pool.dma_start(w2[:], w2_chunks).then_inc(moe_in, 16)
            pool.wait_ge(zeroed, 1)

            def rstd(g):
                pool.wait_ge(ln1_var, g + 1)
                nc.gpsimd.tensor_tensor(rstd1[:], var1[:], half_pow[:, 0:GB], ALU.pow).then_inc(ln1_rstd, 1)

            def expand_k(g, u):
                pool.wait_ge(front_out, g * GB + 1)
                pool.sem_inc(passed, 1)
                for hh in range(HQ):
                    ins = nc.gpsimd.tensor_scalar(k_exp[:, u, :, hh, :], kT[:, u, :, :], head_mask[:, hh:hh + 1], 1.0,
                                                  ALU.mult, ALU.mult)
                ins.then_inc(k_exp_ready, 1)

            def expand_q(g, u):
                pool.wait_ge(front_out, g * GB + 3)
                pool.sem_inc(passed, 1)
                for hh in range(HQ):
                    ins = nc.gpsimd.tensor_scalar(q_exp[:, u, :, hh, :], qT[:, u, :].rearrange("p (b s) -> p b s", b=GB),
                                                  head_mask[:, hh:hh + 1], 1.0, ALU.mult, ALU.mult)
                ins.then_inc(q_exp_ready, 1)

            rstd(0)
            pool.wait_ge(w_in, 7 * 16)
            expand_k(0, 0)
            expand_q(0, 0)

            def slot(i, o):
                gi = o // GB + 1
                if below(i, o, B - GB):
                    if o % GB == 0:
                        rstd(i * 2 + gi)
                        pool.wait_ge(s_done, (i * BODY + o) * 2 - 2 * GB + 2 * GB)
                        expand_k(i * 2 + gi, gi % 2)
                    if o % GB == 2:
                        pool.wait_ge(st_done, (i * BODY + o) * 2 - 4)
                        expand_q(i * 2 + gi, gi % 2)

            walk(pool, slot)
            pool.wait_ge(ln2_var, 1)
            nc.gpsimd.tensor_tensor(rstd2[:], var2[:], half_pow[:], ALU.pow).then_inc(ln2_rstd, 1)
            with pool.Fori(0, NG) as j:
                pool.wait_ge(x2T_out, j + 1)
                pool.sem_inc(passed, 1)
                nc.gpsimd.tensor_copy(xn2T[:, bass.ds(j * GT, GT)], xn2T_buf[:]).then_inc(x2T_kept, 1)

        @block.scalar
        def _(act):
            act.wait_ge(moe_in, 10 * 16)
            nc.scalar.activation(tanh_g[:], gates[:], ACT.Tanh).then_inc(tanh_done, 1)

            def slot(i, o):
                n = i * BODY + o
                if not below(i, o, B):
                    return
                r = o % 2
                act.wait_ge(mT_done, n + 1)
                if o >= 2:
                    act.wait_ge(st_done, n * 2 - 2)
                nc.scalar.activation(m_exp[:, r, :], m_ps, ACT.Copy).then_inc(m_ready, 1)
                for p in range(2):
                    act.wait_ge(st_done, n * 2 + (p + 1))
                    if p == 0 and o >= 2:
                        act.wait_ge(av_done, n - 1)
                    nc.scalar.activation(probs[0:KV, r, p * 1024:(p + 1) * 1024],
                                         st_ps[p][0:KV, :, :].rearrange("k b c -> k (b c)"),
                                         ACT.Exp, scale=SCALE).then_inc(exp_done, 1)

            walk(act, slot)
            with act.Fori(0, NG) as j:
                act.wait_ge(x2T_done, j + 1)
                act.wait_ge(lg_done, j)
                act.wait_ge(x2T_kept, j)
                nc.scalar.activation(xn2T_buf[:], psum[:, 0, :], ACT.Copy).then_inc(x2T_out, 1)
            act.wait_ge(soft_in, 1)
            nc.scalar.activation(wts[:], logits[:], ACT.Exp).then_inc(soft_exp, 1)
            with act.Fori(0, NG) as j:
                for c in range(NCH):
                    act.wait_ge(l1_done, j * NCH + (c + 1))
                    if c >= 2:
                        act.wait_ge(l2_done, j * NCH + (c - 1))
                    else:
                        act.wait_ge(l2_done, j * NCH)
                    nc.scalar.activation(hid[:, c % 2, :], psum[:, c % 2, :], ACT.Gelu,
                                         bias=b1c[:, c:c + 1]).then_inc(gelu_done, 1)

        @block.vector
        def _(dve):
            def front_stats(i, gi):
                g = i * 2 + gi
                dve.wait_ge(x_in, (g + 1) * 32)
                dve.sem_inc(passed, 1)
                for b in range(GB):
                    ins = nc.vector.bn_stats(stats[:, b, :], x_all[:, bass.ds(g * GB + b, 1), :].rearrange("p a d -> p (a d)"))
                return ins

            def xcopy(gi_u, s):
                if s == 0:
                    nc.vector.tensor_copy(kT[:, gi_u, :, :].rearrange("p b k -> p (b k)"), m_ps[:, 0:GB * KV]).then_inc(front_out, 1)
                elif s == 1:
                    nc.vector.tensor_copy(xnT[:], m_ps).then_inc(front_out, 1)
                elif s == 2:
                    nc.vector.tensor_copy(qT[:, gi_u, :], m_ps).then_inc(front_out, 1)
                else:
                    for b in range(GB):
                        dst = v_exp[0:KV, gi_u, b, :].rearrange("k (h c) -> k h c", h=HQ)[:, :, 0:P]
                        dst = dst.rearrange("k h (g c) -> k h g c", g=4)[:, :, :, 0:DK]
                        src = m_ps[0:KV, b * P:(b + 1) * P].rearrange("k (g h c) -> k h g c", g=4, h=HQ)
                        ins = nc.vector.tensor_copy(dst, src)
                    ins.then_inc(front_out, 1)

            def ln1(i, gi):
                g = i * 2 + gi
                front_stats(i, gi).then_inc(ln1_a, 1)
                dve.wait_ge(ln1_a, g + 1)
                dve.sem_inc(passed, 1)
                for b in range(GB):
                    ins = nc.vector.bn_aggr(mv1[:, b, :], stats[:, b, :])
                ins.then_inc(ln1_b, 1)
                dve.wait_ge(ln1_b, g + 1)
                nc.vector.tensor_scalar(var1[:], mv1[:, :, 1:2].rearrange("p b a -> p (b a)"), EPS, None, ALU.add).then_inc(ln1_var, 1)
                dve.wait_ge(ln1_rstd, g + 1)
                for b in range(GB):
                    ins = nc.vector.tensor_scalar(xn[:, b, :], x_all[:, bass.ds(g * GB + b, 1), :].rearrange("p a d -> p (a d)"),
                                                  mv1[:, b, 0:1], rstd1[:, b:b + 1], ALU.subtract, ALU.mult)
                ins.then_inc(xn_ready, 1)

            dve.wait_ge(zeroed, 1)
            ln1(0, 0)
            for s in range(GB):
                dve.wait_ge(front_done, s + 1)
                xcopy(0, s)

            def maxima(i, o):
                n = i * BODY + o
                if o >= 2:
                    dve.wait_ge(mT_done, n - 1)
                for p in range(2):
                    dve.wait_ge(s_done, n * 2 + (p + 1))
                    src = s_ps[:, :, 0:HQ * KV].rearrange("q g (h k) -> q g h k", h=HQ)
                    dst = m_exp_q[:, o % 2, :].rearrange("q (h c) -> q h c", h=HQ)[:, :, 64 * p:64 * p + 64:32]
                    nc.vector.tensor_reduce(dst.rearrange("q h g -> q g h"), src, AX.X, ALU.max).then_inc(max_done, 1)

            def residual(i, o):
                n = i * BODY + o
                dve.wait_ge(wo_done, n + 1)
                tile = x_all[:, bass.ds(n, 1), :].rearrange("p a d -> p (a d)")
                nc.vector.scalar_tensor_tensor(tile, y_ps, tanh_g[:, 0:1], tile, ALU.mult, ALU.add).then_inc(x1_done, 1)
                dve.wait_ge(x1_done, n + 1)
                dve.sem_inc(passed, 1)
                nc.vector.bn_stats(stats2[:, bass.ds(n, 1), :].rearrange("p a d -> p (a d)"), tile).then_inc(stats2_done, 1)

            def normalise(i, o):
                n = i * BODY + o
                dve.wait_ge(av_done, n + 1)
                nc.vector.reciprocal(r_den[:], den_ps).then_inc(rden_done, 1)
                dve.wait_ge(rden_done, n + 1)
                nc.vector.tensor_tensor(onT[:], o_ps, r_den[:], ALU.mult).then_inc(on_ready, 1)

            maxima(0, 0)
            dve.wait_ge(tanh_done, 1)

            def slot(i, o):
                n = i * BODY + o
                if below(i, o + 1, B):
                    maxima(i, o + 1)
                if o >= 2:
                    residual(i, o - 2)
                if below(i, o, B - GB):
                    if o % GB == 0:
                        ln1(i, o // GB + 1)
                    dve.wait_ge(front_done, n + (GB + 1))
                    xcopy((o // GB + 1) % 2, o % GB)
                if o >= 1 and below(i, o, B + 1):
                    normalise(i, o - 1)

            walk(dve, slot)
            dve.wait_ge(stats2_done, B)
            for n in range(B):
                ins = nc.vector.bn_aggr(mv2[:, n, :], stats2[:, n, :])
            ins.then_inc(mv2_done, 1)
            dve.wait_ge(mv2_done, 1)
            nc.vector.tensor_scalar(var2[:], mv2[:, :, 1:2].rearrange("p b a -> p (b a)"), EPS, None, ALU.add).then_inc(ln2_var, 1)
            dve.wait_ge(ln2_rstd, 1)
            with dve.Fori(0, NG) as j:
                dve.wait_ge(x2T_done, j)
                for b in range(GB):
                    ins = nc.vector.tensor_scalar(xn[:, b, :], x_all[:, bass.ds(j * GB + b, 1), :].rearrange("p a d -> p (a d)"),
                                                  mv2[:, bass.ds(j * GB + b, 1), 0:1].rearrange("p a d -> p (a d)"),
                                                  rstd2[:, bass.ds(j * GB + b, 1)], ALU.subtract, ALU.mult)
                ins.then_inc(xn2_ready, 1)
                dve.wait_ge(lg_done, j + 1)
                nc.vector.tensor_tensor(logits[:, bass.ds(j * GB, GB), :],
                                        psum[:, 1, 0:GB * E].rearrange("p (b e) -> p b e", b=GB),
                                        gb_bc[:].unsqueeze(1).broadcast_to([P, GB, E]), ALU.add).then_inc(lg_out, 1)
            cnt = {"n": 0}

            def step(ins):
                cnt["n"] += 1
                ins.then_inc(dve_step, 1)
                dve.wait_ge(dve_step, cnt["n"])

            def over_e(t):
                return t[:].unsqueeze(2).broadcast_to([P, B, E])

            dve.wait_ge(lg_out, NG)
            step(nc.vector.tensor_reduce(red[:], logits[:], AX.X, ALU.max))
            nc.vector.tensor_tensor(logits[:], logits[:], over_e(red), ALU.subtract).then_inc(soft_in, 1)
            dve.wait_ge(soft_exp, 1)
            step(nc.vector.tensor_reduce(red[:], wts[:], AX.X, ALU.add))
            step(nc.vector.reciprocal(red[:], red[:]))
            step(nc.vector.tensor_tensor(gated[:], wts[:], over_e(red), ALU.mult))
            step(nc.vector.tensor_copy(wts[:], gated[:]))
            for _ in range(3):
                step(nc.vector.tensor_reduce(red[:], wts[:], AX.X, ALU.max))
                step(nc.vector.tensor_tensor(pick[:], wts[:], over_e(red), ALU.is_equal))
                step(nc.vector.tensor_tensor(pick[:], pick[:], rev_sb[:].unsqueeze(1).broadcast_to([P, B, E]), ALU.mult))
                step(nc.vector.tensor_reduce(red[:], pick[:], AX.X, ALU.max))
                step(nc.vector.tensor_tensor(pick2[:], pick[:], over_e(red), ALU.is_equal))
                step(nc.vector.scalar_tensor_tensor(wts[:], pick2[:], -2.0, wts[:], ALU.mult, ALU.add))
            step(nc.vector.tensor_scalar(pick[:], wts[:], -0.5, None, ALU.is_lt))
            step(nc.vector.tensor_tensor(gated[:], gated[:], pick[:], ALU.mult))
            nc.vector.drain().then_inc(gated_ready, 1)
            def tokens(t):
                return x_all[:, bass.ds(t, 1), :].rearrange("p a d -> p (a d)")

            with dve.Fori(0, NG // 2) as jj:
                for u in range(2):
                    j = jj * 2 + u
                    nc.vector.tensor_copy(gated_g[:, u, :, :], gated[:, bass.ds(j * GB, GB), :]).then_inc(gates_in, 1)
                    dve.wait_ge(gT_done, j + 1)
                    nc.vector.tensor_copy(gatedT[:], psum[0:E, 4, 0:GT]).then_inc(gT_out, 1)
                    dve.wait_ge(y_out, jj * 32)
                    for b in range(GB):
                        t = j * GB + b
                        ins = nc.vector.tensor_scalar(xn[:, b, :], tokens(t), mv2[:, bass.ds(t, 1), 0:1].rearrange("p a d -> p (a d)"),
                                                      rstd2[:, bass.ds(t, 1)], ALU.subtract, ALU.mult)
                    ins.then_inc(acc_step, 1)
                    dve.wait_ge(acc_step, j * 2 + 1)
                    dve.wait_ge(bias_done, j + 1)
                    nc.vector.tensor_tensor(acc[:, u, :], psum[:, 5, :], xn[:].rearrange("p b d -> p (b d)"), ALU.add).then_inc(acc_step, 1)
                    dve.wait_ge(acc_step, j * 2 + 2)
                    acc_b = acc[:, u, :].rearrange("p (b d) -> p b d", b=GB)
                    nc.vector.tensor_tensor(acc_b, acc_b, sb2_bc[:].unsqueeze(1).broadcast_to([P, GB, D]), ALU.add).then_inc(acc_init, 1)
                    dve.wait_ge(acc_init, j + 1)
                    for e in range(E + 1):
                        dve.wait_ge(l2_done, j * NCH + (CS + e * CR))
                        if e:
                            dve.wait_ge(acc_done, j * (E + 1) + e)
                        for b in range(GB):
                            a = acc[:, u, b * D:(b + 1) * D]
                            y_e = psum[:, 2 + e % 2, b * D:(b + 1) * D]
                            if e == 0:
                                ins = nc.vector.tensor_tensor(a, y_e, a, ALU.add)
                            else:
                                ins = nc.vector.scalar_tensor_tensor(a, y_e, gated_g[:, u, b, e - 1:e], a, ALU.mult, ALU.add)
                        ins.then_inc(acc_done, 1)
                    dve.wait_ge(acc_done, (j + 1) * (E + 1))
                    nc.vector.scalar_tensor_tensor(acc[:, u, :], acc[:, u, :], tanh_g[:, 1:2],
                                                   x_all[:, bass.ds(j * GB, GB), :].rearrange("p a d -> p (a d)"),
                                                   ALU.mult, ALU.add).then_inc(y_ready, 1)

        @block.tensor
        def _(pe):
            def front(i, gi, s, n_sems):
                g = i * 2 + gi
                u = gi % 2
                if s == 0:
                    pe.wait_ge(x_in, (g + 1) * 32)
                    ins = nc.tensor.matmul(m_ps[:, 0:GB * KV], w_kT[:], ctx_buf[:, u, :], start=True, stop=True)
                elif s == 1:
                    pe.wait_ge(xn_ready, g + 1)
                    for b in range(GB):
                        ins = nc.tensor.transpose(m_ps[:, b * S:(b + 1) * S], xn[:, b, :], ident_sb[:])
                elif s == 2:
                    ins = nc.tensor.matmul(m_ps, w_qT[:], xnT[:], start=True, stop=True)
                else:
                    for b in range(GB):
                        ins = nc.tensor.matmul(m_ps[0:KV, b * P:(b + 1) * P], ctx_buf[:, u, b * KV:(b + 1) * KV], w_vT[:],
                                               start=True, stop=True)
                ins.then_inc(front_done, 1)

            def scores(i, o):
                n = i * BODY + o
                u, b = o // GB % 2, o % GB
                if b == 0:
                    pe.wait_ge(k_exp_ready, i * 2 + (o // GB + 1))
                    pe.wait_ge(front_out, i * BODY + (o + 3))
                for p in range(2):
                    pe.wait_ge(max_done, n * 2 + p)
                    for j in range(2):
                        r = 64 * p + 32 * j
                        ins = nc.tensor.matmul(s_ps[:, j, 0:HQ * KV], qT[r:r + 32, u, b * S:(b + 1) * S],
                                               k_exp[r:r + 32, u, b, :, :].rearrange("p h k -> p (h k)"), start=True, stop=True)
                    ins.then_inc(s_done, 1)

            def spread_max(i, o):
                n = i * BODY + o
                pe.wait_ge(max_done, n * 2 + 2)
                pe.wait_ge(front_out, n + GB)
                for hh in range(HQ):
                    ins = nc.tensor.transpose(m_ps[:, hh * S:(hh + 1) * S], m_exp_q[:, o % 2, hh * P:(hh + 1) * P], ident_sb[:])
                ins.then_inc(mT_done, 1)

            def scores_t(i, o):
                n = i * BODY + o
                u, b = o // GB % 2, o % GB
                if b == 0:
                    pe.wait_ge(q_exp_ready, i * 2 + (o // GB + 1))
                for p in range(2):
                    if o >= 1:
                        pe.wait_ge(exp_done, n * 2 + (p - 1))
                    for j in range(2):
                        r = 64 * p + 32 * j
                        nc.tensor.matmul(st_ps[p][0:KV, j, :], kT[r:r + 32, u, b, :],
                                         q_exp[r:r + 32, u, b, :, :].rearrange("p h s -> p (h s)"), start=True, stop=False)
                    pe.wait_ge(m_ready, n + 1)
                    for j in range(2):
                        r = 64 * p + 32 * j
                        ins = nc.tensor.matmul(st_ps[p][0:KV, j, :], neg_ones[r:r + 32, :], m_exp[r:r + 32, o % 2, :],
                                               start=False, stop=True)
                    ins.then_inc(st_done, 1)

            def values(i, o):
                n = i * BODY + o
                u, b = o // GB % 2, o % GB
                pe.wait_ge(exp_done, n * 2 + 2)
                if o >= 1:
                    pe.wait_ge(x1_done, n)
                vb = v_exp[0:KV, u, b, :]
                for dst, den in ((o_ps, False), (den_ps, True)):
                    for hh in range(HQ):
                        for j in range(4):
                            h = j * HQ + hh
                            lhs = den_lhs[0:KV, hh, :] if den else vb[:, hh * P + 32 * j:hh * P + 32 * j + 32]
                            ins = nc.tensor.matmul(dst[32 * j:32 * j + 32, :], lhs, probs[0:KV, o % 2, h * S:(h + 1) * S],
                                                   start=(hh == 0), stop=(hh == HQ - 1), tile_position=(0, 32 * j))
                ins.then_inc(av_done, 1)

            def project(i, o):
                n = i * BODY + o
                pe.wait_ge(on_ready, n + 1)
                nc.tensor.matmul(y_ps, onT[:], w_oT[:], start=True, stop=True).then_inc(wo_done, 1)

            pe.wait_ge(w_in, 7 * 16)
            pe.wait_ge(zeroed, 1)
            for s in range(GB):
                if s:
                    pe.wait_ge(front_out, s)
                front(0, 0, s, s)
            pe.wait_ge(front_out, GB)
            scores(0, 0)

            def slot(i, o):
                n = i * BODY + o
                if below(i, o + 1, B):
                    scores(i, o + 1)
                if o >= 2:
                    project(i, o - 2)
                if below(i, o, B):
                    if not below(i, o, B - GB + 1):
                        spread_max_tail(i, o)
                    else:
                        spread_max(i, o)
                    scores_t(i, o)
                if below(i, o, B - GB):
                    pe.wait_ge(m_ready, n + 1)
                    front(i, o // GB + 1, o % GB, None)
                if o >= 1 and below(i, o, B + 1):
                    values(i, o - 1)

            def spread_max_tail(i, o):
                n = i * BODY + o
                pe.wait_ge(max_done, n * 2 + 2)
                pe.wait_ge(m_ready, n)
                for hh in range(HQ):
                    ins = nc.tensor.transpose(m_ps[:, hh * S:(hh + 1) * S], m_exp_q[:, o % 2, hh * P:(hh + 1) * P], ident_sb[:])
                ins.then_inc(mT_done, 1)

            walk(pe, slot)
            pe.wait_ge(moe_in, 10 * 16)
            with pe.Fori(0, NG) as j:
                pe.wait_ge(xn2_ready, j + 1)
                pe.wait_ge(x2T_out, j)
                for b in range(GB):
                    ins = nc.tensor.transpose(psum[:, 0, b * S:(b + 1) * S], xn[:, b, :], ident_sb[:])
                ins.then_inc(x2T_done, 1)
                pe.wait_ge(x2T_out, j + 1)
                pe.wait_ge(lg_out, j)
                for b in range(GB):
                    ins = nc.tensor.matmul(psum[:, 1, b * E:(b + 1) * E], xn2T_buf[:, b * S:(b + 1) * S], gw_sb[:],
                                           start=True, stop=True)
                ins.then_inc(lg_done, 1)
            pe.wait_ge(x2T_kept, NG)
            pe.wait_ge(gated_ready, 1)
            def gate_bias(j, u):
                pe.wait_ge(gates_in, j + 1)
                pe.wait_ge(gT_out, j)
                for b in range(GB):
                    ins = nc.tensor.transpose(psum[0:E, 4, b * S:(b + 1) * S], gated_g[:, u, b, :], ident_sb[:])
                ins.then_inc(gT_done, 1)
                pe.wait_ge(gT_out, j + 1)
                pe.wait_ge(acc_init, j)
                for b in range(GB):
                    ins = nc.tensor.matmul(psum[:, 5, b * D:(b + 1) * D], gatedT[:, b * S:(b + 1) * S], b2row[:],
                                           start=True, stop=True)
                ins.then_inc(bias_done, 1)

            def layer1(j, c):
                if c >= 2:
                    pe.wait_ge(gelu_done, j * NCH + (c - 1))
                else:
                    pe.wait_ge(gelu_done, j * NCH)
                nc.tensor.matmul(psum[:, c % 2, :], w1[:, c, :], xn2T[:, bass.ds(j * GT, GT)],
                                 start=True, stop=True).then_inc(l1_done, 1)

            def layer2(j, c):
                e, first, last = (0, c == 0, c == CS - 1) if c < CS else \
                    ((c - CS) // CR + 1, (c - CS) % CR == 0, (c - CS) % CR == CR - 1)
                pe.wait_ge(gelu_done, j * NCH + (c + 1))
                if first and e >= 2:
                    pe.wait_ge(acc_done, j * (E + 1) + (e - 1))
                elif first:
                    pe.wait_ge(acc_done, j * (E + 1))
                for b in range(GB):
                    ins = nc.tensor.matmul(psum[:, 2 + e % 2, b * D:(b + 1) * D], hid[:, c % 2, b * S:(b + 1) * S], w2[:, c, :],
                                           start=first and b == 0, stop=last, skip_group_check=True)
                ins.then_inc(l2_done, 1)

            with pe.Fori(0, NG // 2) as jj:
                for u in range(2):
                    j = jj * 2 + u
                    layer1(j, 0)
                    gate_bias(j, u)
                    for c in range(NCH):
                        if c + 1 < NCH:
                            layer1(j, c + 1)
                        layer2(j, c)


_INS = ["x", "ctxT", "g_xattn", "g_ffn", "wqT", "wkT", "wvT", "woT", "w1_chunks", "b1_cols", "w2_chunks", "sb2",
        "rb2", "gW", "gb", "ident", "head_of_row", "den_sel", "rev_idx"]


def kernel(**inputs):
    import numpy as np
    import concourse.bacc as bacc
    from concourse.bass_utils import run_bass_kernel_spmd

    data = {k.replace("L0_xattn_", "").replace("L0_ffn_", ""): np.asarray(v) for k, v in inputs.items()}
    ctx = data.pop("ctx_1024")
    data["ctxT"] = ctx.transpose(2, 0, 1).reshape(ctx.shape[2], -1)
    for n in "qkvo":
        data[f"w{n}T"] = data.pop(f"w_{n}").T
    d = data["sW1"].shape[1]
    data["w1_chunks"] = np.concatenate(
        [w.reshape(len(w), d, -1, P).transpose(1, 0, 2, 3).reshape(d, -1, P) for w in (data["sW1"], data["rW1"])], axis=1)
    data["w2_chunks"] = np.concatenate([w.reshape(-1, P, d).transpose(1, 0, 2) for w in (data["sW2"], data["rW2"])], axis=1)
    data["b1_cols"] = np.concatenate([b.reshape(-1, P) for b in (data["sb1"], data["rb1"])]).T
    rows = np.arange(P)
    heads = rows // 8 % 4
    data["ident"] = np.eye(P, dtype=np.float32)
    data["head_of_row"] = (heads[:, None] == np.arange(4)[None]).astype(np.float32)
    sel = (np.arange(32)[None] // 8 == np.arange(4)[:, None]).astype(np.float32)
    data["den_sel"] = np.broadcast_to(sel, (P, 4, 32))
    experts = data["gW"].shape[1]
    data["rev_idx"] = np.broadcast_to(experts - np.arange(experts, dtype=np.float32), (P, experts))

    nc = bacc.Bacc("TRN2", target_bir_lowering=False, num_devices=1)
    arrays, args = {}, []
    for name in _INS:
        a = np.ascontiguousarray(data[name])
        arrays[f"in_{name}"] = a
        args.append(nc.dram_tensor(f"in_{name}", a.shape, mybir.dt.from_np(a.dtype), kind="ExternalInput").ap())
    shape = data["x"].shape
    args.append(nc.dram_tensor("out_0", shape, F32, kind="ExternalOutput").ap())
    flamingo_kernel(nc, *args)
    r = run_bass_kernel_spmd(nc, [arrays], core_ids=[0])
    return r.results[0]["out_0"]
```

```python
from contextlib import ExitStack

import concourse.bass as bass
from concourse import mybir

P = 128
F32 = mybir.dt.float32
F32R = mybir.dt.float32r
ALU = mybir.AluOpType
ACT = mybir.ActivationFunctionType
AX = mybir.AxisListType
EPS = 1e-5


def flamingo_kernel(nc, x, ctxT, g_xattn, g_ffn, wqT3, wkT3, wvT, woT, w1_chunks, b1_cols, w2_chunks, sb2,
                    rb2, gW, gb, ident, head_of_row, rev_idx, out):
    B, S, D = x.shape
    KP = ctxT.shape[1] // B
    KV = KP - 1
    H, DK = 16, 8
    HQ = P // DK // 4
    GB = 4
    NG = B // GB
    GT = GB * S
    E = gW.shape[1]
    NCH = w1_chunks.shape[1]
    CR, CS = 2, 4
    assert NCH == CS + E * CR
    SCALE = float(DK) ** -0.5
    BODY = 2 * GB
    LEAD = 2
    HG = H // HQ
    KS = 3 * HQ * DK
    HH = H // 2
    VB = HH * (P + DK) + P // 2
    NF = 10
    PIECES = ((0, 1, 2), (3, 4, 5), (6, 7, 8), (9,))

    with ExitStack() as ctx:
        def sb(name, shape, dt=F32):
            return ctx.enter_context(nc.sbuf_tensor(name, shape, dt))

        def sem(name):
            return ctx.enter_context(nc.semaphore(name))

        x_all = sb("x_all", [P, B, D])
        ctx_buf = sb("ctx_buf", [P, 2, GB * KP])
        w_q3, w_k3 = (sb(n, [P, HG, KS]) for n in ("w_q3", "w_k3"))
        w_vT, w_oT = (sb(n, [P, P]) for n in ("w_vT", "w_oT"))
        w1 = sb("w1", [P, NCH, P])
        w2 = sb("w2", [P, NCH, P])
        b1c = sb("b1c", [P, NCH])
        b2row = sb("b2row", [E, D])
        sb2_bc = sb("sb2_bc", [P, D])
        gw_sb = sb("gw_sb", [P, E])
        gb_bc = sb("gb_bc", [P, E])
        ident_sb = sb("ident_sb", [P, P])
        head_mask = sb("head_mask", [P, HQ])
        rev_sb = sb("rev_sb", [P, E])
        half_pow = sb("half_pow", [P, B])
        gates = sb("gates", [P, 2])
        tanh_g = sb("tanh_g", [P, 2])
        stats = sb("stats", [P, GB, 6])
        mv1 = sb("mv1", [P, GB, 2])
        var1 = sb("var1", [P, GB])
        rstd1 = sb("rstd1", [P, GB])
        xn = sb("xn", [P, GB, D])
        xnT = sb("xnT", [P, GT])
        q_stack = sb("q_stack", [P, 2, HG, GT], F32R)
        k_stack = sb("k_stack", [P, HG, GB * KP])
        k_heads = sb("k_heads", [P, 2, HG, HQ, GB * KP], F32R)
        max_cols = sb("max_cols", [P, 2, HG, KS + HQ], F32R)
        ident_r = sb("ident_r", [P, P], F32R)
        v_all = sb("v_all", [P, 2, GT])
        v_den = sb("v_den", [P, 2, 2, VB])
        probs = sb("probs", [P, 2, H * S])
        r_den = sb("r_den", [P, S])
        onT = sb("onT", [P, S])
        stats2 = sb("stats2", [P, B, 6])
        mv2 = sb("mv2", [P, B, 2])
        var2 = sb("var2", [P, B])
        rstd2 = sb("rstd2", [P, B])
        xn2T = sb("xn2T", [P, B * S])
        xn2T_buf = sb("xn2T_buf", [P, GT])
        logits = sb("logits", [P, B, E])
        wts = sb("wts", [P, B, E])
        pick = sb("pick", [P, B, E])
        pick2 = sb("pick2", [P, B, E])
        red = sb("red", [P, B])
        gated = sb("gated", [P, B, E])
        gated_g = sb("gated_g", [P, 2, GB, E])
        gatedT = sb("gatedT", [E, GT])
        hid = probs[:, 0, 0:2 * GT].rearrange("p (r t) -> p r t", r=2)
        acc = probs[:, 1, 0:2 * GT].rearrange("p (r t) -> p r t", r=2)

        psum = ctx.enter_context(nc.psum_tensor("psum", [P, 8, 512], F32))
        s_ps = [psum[:, 0, :], psum[:, 1, :]]
        st_ps = [psum[:, 2, :], psum[:, 3, :]]
        m_ps = psum[:, 4, :]
        y_ps = psum[:, 4, 0:D]
        f_ps = [psum[:, 5, :], psum[:, 6, :]]
        o_ps = [psum[:, 7, 0:S], psum[:, 7, S:2 * S]]

        passed = sem("passed")
        w_in = sem("w_in")
        x_in = sem("x_in")
        moe_in = sem("moe_in")
        zeroed = sem("zeroed")
        fill_zeroed = sem("fill_zeroed")
        tanh_done = sem("tanh_done")
        ln1_var = sem("ln1_var")
        ln1_rstd = sem("ln1_rstd")
        xn_ready = sem("xn_ready")
        front_done = sem("front_done")
        front_out = sem("front_out")
        front_hi = sem("front_hi")
        k_heads_ready = sem("k_heads_ready")
        v_den_ready = sem("v_den_ready")
        id_ready = sem("id_ready")
        s_done = sem("s_done")
        max_done = sem("max_done")
        mT_done = sem("mT_done")
        m_ready = sem("m_ready")
        st_done = sem("st_done")
        exp_done = sem("exp_done")
        av_done = sem("av_done")
        rden_done = sem("rden_done")
        on_ready = sem("on_ready")
        wo_done = sem("wo_done")
        x1_done = sem("x1_done")
        dve_step = sem("dve_step")

        ln2_var = sem("ln2_var")
        ln2_rstd = sem("ln2_rstd")
        xn2_ready = sem("xn2_ready")
        x2T_done = sem("x2T_done")
        x2T_out = sem("x2T_out")
        x2T_kept = sem("x2T_kept")
        lg_done = sem("lg_done")
        lg_out = sem("lg_out")
        soft_in = sem("soft_in")
        soft_exp = sem("soft_exp")
        gated_ready = sem("gated_ready")
        ln1_a = sem("ln1_a")
        ln1_b = sem("ln1_b")
        stats2_done = sem("stats2_done")
        mv2_done = sem("mv2_done")
        gates_in = sem("gates_in")
        acc_step = sem("acc_step")
        gT_done = sem("gT_done")
        gT_out = sem("gT_out")
        bias_done = sem("bias_done")
        acc_init = sem("acc_init")
        l1_done = sem("l1_done")
        gelu_done = sem("gelu_done")
        l2_done = sem("l2_done")
        acc_done = sem("acc_done")
        y_ready = sem("y_ready")
        y_out = sem("y_out")

        block = ctx.enter_context(nc.Block())

        def walk(eng, slot):
            for o in range(LEAD):
                slot(0, o)
            with eng.Fori(0, NG // 2 - 1) as i:
                for o in range(LEAD, LEAD + BODY):
                    slot(i, o)
            for o in range(LEAD, BODY + 2):
                slot(NG // 2 - 1, o)

        def below(i, o, limit):
            return not isinstance(i, int) or i * BODY + o < limit

        @block.sync
        def _(sp):
            for dst, src in ((w_q3, wqT3), (w_k3, wkT3), (w_vT, wvT), (w_oT, woT), (ident_sb, ident),
                             (head_mask, head_of_row)):
                sp.dma_start(dst[:], src).then_inc(w_in, 16)

            def load_group(i, u):
                g = i * 2 + u
                sp.wait_ge(x_in, g * 32)
                sp.sem_inc(passed, 1)
                if not isinstance(i, int) or i > 0:
                    sp.wait_ge(front_out, (i * 2 + (u - 1)) * NF)
                    sp.sem_inc(passed, 1)
                sp.dma_start(x_all[:, bass.ds(g * GB, GB), :],
                             x[bass.ds(g * GB, GB), :, :].rearrange("b t d -> t b d")).then_inc(x_in, 16)
                sp.dma_start(ctx_buf[:, u, :], ctxT[:, bass.ds(g * (GB * KP), GB * KP)]).then_inc(x_in, 16)

            for u in range(2):
                load_group(0, u)
            with sp.Fori(1, NG // 2) as i:
                for u in range(2):
                    load_group(i, u)
            with sp.Fori(0, NG // 2) as j:
                for u in range(2):
                    sp.wait_ge(y_ready, j * 2 + (u + 1))
                    sp.dma_start(out[bass.ds((j * 2 + u) * GB, GB), :, :].rearrange("b t d -> t b d"),
                                 acc[:, u, :].rearrange("p (b d) -> p b d", b=GB)).then_inc(y_out, 16)
                    sp.wait_ge(y_out, j * 32 + (u + 1) * 16)
                    sp.sem_inc(passed, 1)

        @block.gpsimd
        def _(pool):
            pool.memset(max_cols[:].bitcast(F32), 0.0)
            pool.memset(k_stack[:], -1.0)
            pool.memset(v_den[:], 0.0).then_inc(zeroed, 1)
            pool.memset(half_pow[:], -0.5)
            pool.wait_ge(zeroed, 1)
            for r in range(2):
                for p in range(2):
                    ones = v_den[:, r, p, (1 - p) * 64:(1 - p) * 64 + HH * (P + DK)].rearrange("k (h c) -> k h c", h=HH)[:, :, 0:DK]
                    ins = pool.memset(ones, 1.0)
            ins.then_inc(zeroed, 1)
            pool.dma_start(gates[:, 0:1], g_xattn.rearrange("(a b) -> a b", a=1).partition_broadcast(P)).then_inc(moe_in, 16)
            pool.dma_start(gates[:, 1:2], g_ffn.rearrange("(a b) -> a b", a=1).partition_broadcast(P)).then_inc(moe_in, 16)
            pool.dma_start(sb2_bc[:], sb2.partition_broadcast(P)).then_inc(moe_in, 16)
            pool.dma_start(gb_bc[:], gb.rearrange("(a e) -> a e", a=1).partition_broadcast(P)).then_inc(moe_in, 16)
            pool.dma_start(rev_sb[:], rev_idx).then_inc(moe_in, 16)
            pool.dma_start(gw_sb[:], gW).then_inc(moe_in, 16)
            pool.dma_start(b2row[:], rb2).then_inc(moe_in, 16)
            pool.dma_start(b1c[:], b1_cols).then_inc(moe_in, 16)
            pool.dma_start(w1[:], w1_chunks).then_inc(moe_in, 16)
            pool.dma_start(w2[:], w2_chunks).then_inc(moe_in, 16)
            pool.wait_ge(zeroed, 2)

            def rstd(g):
                pool.wait_ge(ln1_var, g + 1)
                nc.gpsimd.tensor_tensor(rstd1[:], var1[:], half_pow[:, 0:GB], ALU.pow).then_inc(ln1_rstd, 1)

            def expand_k(g, u):
                pool.wait_ge(front_out, g * NF + 5)
                pool.sem_inc(passed, 1)
                for hh in range(HQ):
                    ins = nc.gpsimd.tensor_scalar(k_heads[:, u, :, hh, :], k_stack[:], head_mask[:, hh:hh + 1], 1.0, ALU.mult, ALU.mult)
                ins.then_inc(k_heads_ready, 1)

            def place_v(i, o):
                n = i * BODY + o
                u, b = o // GB % 2, o % GB
                pool.wait_ge(front_out, (i * 2 + (o // GB + 1)) * NF)
                pool.sem_inc(passed, 1)
                if o >= 2:
                    pool.wait_ge(av_done, n * 2 - 2)
                    pool.sem_inc(passed, 1)
                for p in range(2):
                    dst = v_den[0:KV, o % 2, p, p * 64:p * 64 + HH * (P + DK)].rearrange("k (h c) -> k h c", h=HH)[:, :, 0:DK]
                    src = v_all[0:KV, u, b * P + p * 64:b * P + p * 64 + 64].rearrange("k (h c) -> k h c", h=HH)
                    ins = nc.gpsimd.tensor_copy(dst, src)
                ins.then_inc(v_den_ready, 1)

            rstd(0)
            pool.wait_ge(w_in, 6 * 16)
            expand_k(0, 0)
            rstd(1)

            def slot(i, o):
                if below(i, o, B):
                    place_v(i, o)
                if o % GB == 1 and below(i, o, B - GB):
                    expand_k(i * 2 + o // GB + 1, (o // GB + 1) % 2)
                if o % GB == 3 and below(i, o, B - 2 * GB):
                    rstd(i * 2 + o // GB + 2)

            walk(pool, slot)
            pool.wait_ge(ln2_var, 1)
            nc.gpsimd.tensor_tensor(rstd2[:], var2[:], half_pow[:], ALU.pow).then_inc(ln2_rstd, 1)
            with pool.Fori(0, NG) as j:
                pool.wait_ge(x2T_out, j + 1)
                pool.sem_inc(passed, 1)
                nc.gpsimd.tensor_copy(xn2T[:, bass.ds(j * GT, GT)], xn2T_buf[:]).then_inc(x2T_kept, 1)

        @block.scalar
        def _(act):
            act.wait_ge(moe_in, 10 * 16)
            nc.scalar.activation(tanh_g[:], gates[:], ACT.Tanh).then_inc(tanh_done, 1)

            def leading(idx, g_ps, dst):
                act.wait_ge(front_done, idx + 1)
                nc.scalar.activation(dst, g_ps, ACT.Copy).then_inc(front_hi, 1)

            def front_leading(i, gi, j):
                idx = (i * 2 + gi) * NF + j
                u = gi % 2
                if 1 <= j < 5:
                    leading(idx, f_ps[j % 2][0:KS, 0:GB * KP], k_stack[0:KS, j - 1, :].bitcast(F32R))
                elif 5 <= j < 9:
                    leading(idx, f_ps[j % 2][0:KS, :], q_stack[0:KS, u, j - 5, :])

            act.wait_ge(zeroed, 2)
            act.wait_ge(fill_zeroed, 2)
            for j in range(NF):
                front_leading(0, 0, j)

            def max_rows(i, o):
                u, b = o // GB % 2, o % GB
                act.wait_ge(mT_done, i * BODY + (o + 1))
                nc.scalar.activation(q_stack[KS:KS + HQ, u, :, b * S:(b + 1) * S],
                                     m_ps[KS:KS + HQ, :].rearrange("r (g s) -> r g s", g=HG), ACT.Copy).then_inc(m_ready, 1)

            def exps(i, o, g):
                n = i * BODY + o
                act.wait_ge(st_done, n * 4 + (g + 1))
                if g == 0 and o >= 2:
                    act.wait_ge(av_done, n * 2 - 2)
                nc.scalar.activation(probs[0:KV, o % 2, g * 512:(g + 1) * 512], st_ps[g % 2][0:KV, :],
                                     ACT.Exp, scale=SCALE).then_inc(exp_done, 1)

            def slot(i, o):
                fr = PIECES[o % GB] if below(i, o, B - GB) else ()
                if below(i, o, B):
                    max_rows(i, o)
                    exps(i, o, 0)
                    exps(i, o, 1)
                for j in fr[0:1]:
                    front_leading(i, o // GB + 1, j)
                if below(i, o, B):
                    exps(i, o, 2)
                    exps(i, o, 3)
                for j in fr[1:]:
                    front_leading(i, o // GB + 1, j)

            walk(act, slot)
            with act.Fori(0, NG) as j:
                act.wait_ge(x2T_done, j + 1)
                act.wait_ge(lg_done, j)
                act.wait_ge(x2T_kept, j)
                nc.scalar.activation(xn2T_buf[:], psum[:, 0, :], ACT.Copy).then_inc(x2T_out, 1)
            act.wait_ge(soft_in, 1)
            nc.scalar.activation(wts[:], logits[:], ACT.Exp).then_inc(soft_exp, 1)
            with act.Fori(0, NG) as j:
                for c in range(NCH):
                    act.wait_ge(l1_done, j * NCH + (c + 1))
                    if c >= 2:
                        act.wait_ge(l2_done, j * NCH + (c - 1))
                    else:
                        act.wait_ge(l2_done, j * NCH)
                    nc.scalar.activation(hid[:, c % 2, :], psum[:, c % 2, :], ACT.Gelu,
                                         bias=b1c[:, c:c + 1]).then_inc(gelu_done, 1)

        @block.vector
        def _(dve):
            def front_stats(i, gi):
                g = i * 2 + gi
                dve.wait_ge(x_in, (g + 1) * 32)
                dve.sem_inc(passed, 1)
                for b in range(GB):
                    ins = nc.vector.bn_stats(stats[:, b, :], x_all[:, bass.ds(g * GB + b, 1), :].rearrange("p a d -> p (a d)"))
                return ins

            def front_copy(i, gi, j):
                g = i * 2 + gi
                u = gi % 2
                ps = f_ps[j % 2]
                dve.wait_ge(front_done, g * NF + (j + 1))
                if j == 0:
                    nc.vector.tensor_copy(xnT[:], ps).then_inc(front_out, 1)
                elif j < 5:
                    dve.wait_ge(front_hi, g * 8 + j)
                    rows = k_stack[64:96, j - 1, :]
                    nc.vector.tensor_tensor(rows.bitcast(F32R), ps[64:96, 0:GB * KP], rows, ALU.subtract).then_inc(front_out, 1)
                elif j < 9:
                    dve.wait_ge(front_hi, g * 8 + j)
                    rows = q_stack[32:64, u, j - 5, :]
                    nc.vector.tensor_tensor(rows, ps[32:64, :], rows.bitcast(F32), ALU.subtract).then_inc(front_out, 1)
                else:
                    nc.vector.tensor_copy(v_all[0:KV, u, :], ps[0:KV, :]).then_inc(front_out, 1)

            def ln1(i, gi):
                g = i * 2 + gi
                front_stats(i, gi).then_inc(ln1_a, 1)
                dve.wait_ge(ln1_a, g + 1)
                dve.sem_inc(passed, 1)
                for b in range(GB):
                    ins = nc.vector.bn_aggr(mv1[:, b, :], stats[:, b, :])
                ins.then_inc(ln1_b, 1)
                dve.wait_ge(ln1_b, g + 1)
                nc.vector.tensor_scalar(var1[:], mv1[:, :, 1:2].rearrange("p b a -> p (b a)"), EPS, None, ALU.add).then_inc(ln1_var, 1)
                dve.wait_ge(ln1_rstd, g + 1)
                for b in range(GB):
                    ins = nc.vector.tensor_scalar(xn[:, b, :], x_all[:, bass.ds(g * GB + b, 1), :].rearrange("p a d -> p (a d)"),
                                                  mv1[:, b, 0:1], rstd1[:, b:b + 1], ALU.subtract, ALU.mult)
                ins.then_inc(xn_ready, 1)

            nc.vector.memset(q_stack[KS:P, :, :, :].bitcast(F32), 0.0).then_inc(fill_zeroed, 1)
            nc.vector.memset(probs[64:P, :, :], 0.0).then_inc(fill_zeroed, 1)
            dve.wait_ge(zeroed, 2)
            dve.wait_ge(w_in, 6 * 16)
            nc.vector.tensor_copy(ident_r[:], ident_sb[:]).then_inc(id_ready, 1)
            ln1(0, 0)
            for j in range(NF):
                front_copy(0, 0, j)
            ln1(0, 1)

            def maxima(i, o, g):
                n = i * BODY + o
                if o >= 2 and g == 0:
                    dve.wait_ge(mT_done, n - 1)
                dve.wait_ge(s_done, n * 4 + (g + 1))
                nc.vector.tensor_reduce(max_cols[:, o % 2, g, KS:KS + HQ],
                                        s_ps[g % 2][:, 0:HQ * KP].rearrange("q (h k) -> q h k", h=HQ), AX.X, ALU.max).then_inc(max_done, 1)

            def residual(i, o):
                n = i * BODY + o
                dve.wait_ge(wo_done, n + 1)
                tile = x_all[:, bass.ds(n, 1), :].rearrange("p a d -> p (a d)")
                nc.vector.scalar_tensor_tensor(tile, y_ps, tanh_g[:, 0:1], tile, ALU.mult, ALU.add).then_inc(x1_done, 1)
                dve.wait_ge(x1_done, n + 1)
                dve.sem_inc(passed, 1)
                nc.vector.bn_stats(stats2[:, bass.ds(n, 1), :].rearrange("p a d -> p (a d)"), tile).then_inc(stats2_done, 1)

            def normalise(i, o):
                n = i * BODY + o
                dve.wait_ge(av_done, n * 2 + 2)
                nc.vector.reciprocal(r_den[0:64, :], o_ps[0][64:128, :])
                nc.vector.reciprocal(r_den[64:128, :], o_ps[1][0:64, :]).then_inc(rden_done, 1)
                dve.wait_ge(rden_done, n + 1)
                nc.vector.tensor_tensor(onT[0:64, :], o_ps[0][0:64, :], r_den[0:64, :], ALU.mult)
                nc.vector.tensor_tensor(onT[64:128, :], o_ps[1][64:128, :], r_den[64:128, :], ALU.mult).then_inc(on_ready, 1)

            for g in range(HG):
                maxima(0, 0, g)
            dve.wait_ge(tanh_done, 1)

            def slot(i, o):
                fr = PIECES[o % GB] if below(i, o, B - GB) else ()
                if below(i, o + 1, B):
                    maxima(i, o + 1, 0)
                    maxima(i, o + 1, 1)
                if o >= 2:
                    residual(i, o - 2)
                for j in fr[0:2]:
                    front_copy(i, o // GB + 1, j)
                if below(i, o + 1, B):
                    maxima(i, o + 1, 2)
                    maxima(i, o + 1, 3)
                for j in fr[2:]:
                    front_copy(i, o // GB + 1, j)
                if o % GB == 3 and below(i, o, B - 2 * GB):
                    ln1(i, o // GB + 2)
                if o >= 1 and below(i, o, B + 1):
                    normalise(i, o - 1)

            walk(dve, slot)
            dve.wait_ge(stats2_done, B)
            for n in range(B):
                ins = nc.vector.bn_aggr(mv2[:, n, :], stats2[:, n, :])
            ins.then_inc(mv2_done, 1)
            dve.wait_ge(mv2_done, 1)
            nc.vector.tensor_scalar(var2[:], mv2[:, :, 1:2].rearrange("p b a -> p (b a)"), EPS, None, ALU.add).then_inc(ln2_var, 1)
            dve.wait_ge(ln2_rstd, 1)
            with dve.Fori(0, NG) as j:
                dve.wait_ge(x2T_done, j)
                for b in range(GB):
                    ins = nc.vector.tensor_scalar(xn[:, b, :], x_all[:, bass.ds(j * GB + b, 1), :].rearrange("p a d -> p (a d)"),
                                                  mv2[:, bass.ds(j * GB + b, 1), 0:1].rearrange("p a d -> p (a d)"),
                                                  rstd2[:, bass.ds(j * GB + b, 1)], ALU.subtract, ALU.mult)
                ins.then_inc(xn2_ready, 1)
                dve.wait_ge(lg_done, j + 1)
                nc.vector.tensor_tensor(logits[:, bass.ds(j * GB, GB), :],
                                        psum[:, 1, 0:GB * E].rearrange("p (b e) -> p b e", b=GB),
                                        gb_bc[:].unsqueeze(1).broadcast_to([P, GB, E]), ALU.add).then_inc(lg_out, 1)
            cnt = {"n": 0}

            def step(ins):
                cnt["n"] += 1
                ins.then_inc(dve_step, 1)
                dve.wait_ge(dve_step, cnt["n"])

            def over_e(t):
                return t[:].unsqueeze(2).broadcast_to([P, B, E])

            dve.wait_ge(lg_out, NG)
            step(nc.vector.tensor_reduce(red[:], logits[:], AX.X, ALU.max))
            nc.vector.tensor_tensor(logits[:], logits[:], over_e(red), ALU.subtract).then_inc(soft_in, 1)
            dve.wait_ge(soft_exp, 1)
            step(nc.vector.tensor_reduce(red[:], wts[:], AX.X, ALU.add))
            step(nc.vector.reciprocal(red[:], red[:]))
            step(nc.vector.tensor_tensor(gated[:], wts[:], over_e(red), ALU.mult))
            step(nc.vector.tensor_copy(wts[:], gated[:]))
            for _ in range(3):
                step(nc.vector.tensor_reduce(red[:], wts[:], AX.X, ALU.max))
                step(nc.vector.tensor_tensor(pick[:], wts[:], over_e(red), ALU.is_equal))
                step(nc.vector.tensor_tensor(pick[:], pick[:], rev_sb[:].unsqueeze(1).broadcast_to([P, B, E]), ALU.mult))
                step(nc.vector.tensor_reduce(red[:], pick[:], AX.X, ALU.max))
                step(nc.vector.tensor_tensor(pick2[:], pick[:], over_e(red), ALU.is_equal))
                step(nc.vector.scalar_tensor_tensor(wts[:], pick2[:], -2.0, wts[:], ALU.mult, ALU.add))
            step(nc.vector.tensor_scalar(pick[:], wts[:], -0.5, None, ALU.is_lt))
            step(nc.vector.tensor_tensor(gated[:], gated[:], pick[:], ALU.mult))
            nc.vector.drain().then_inc(gated_ready, 1)
            def tokens(t):
                return x_all[:, bass.ds(t, 1), :].rearrange("p a d -> p (a d)")

            with dve.Fori(0, NG // 2) as jj:
                for u in range(2):
                    j = jj * 2 + u
                    nc.vector.tensor_copy(gated_g[:, u, :, :], gated[:, bass.ds(j * GB, GB), :]).then_inc(gates_in, 1)
                    dve.wait_ge(gT_done, j + 1)
                    nc.vector.tensor_copy(gatedT[:], psum[0:E, 4, 0:GT]).then_inc(gT_out, 1)
                    dve.wait_ge(y_out, jj * 32)
                    for b in range(GB):
                        t = j * GB + b
                        ins = nc.vector.tensor_scalar(xn[:, b, :], tokens(t), mv2[:, bass.ds(t, 1), 0:1].rearrange("p a d -> p (a d)"),
                                                      rstd2[:, bass.ds(t, 1)], ALU.subtract, ALU.mult)
                    ins.then_inc(acc_step, 1)
                    dve.wait_ge(acc_step, j * 2 + 1)
                    dve.wait_ge(bias_done, j + 1)
                    nc.vector.tensor_tensor(acc[:, u, :], psum[:, 5, :], xn[:].rearrange("p b d -> p (b d)"), ALU.add).then_inc(acc_step, 1)
                    dve.wait_ge(acc_step, j * 2 + 2)
                    acc_b = acc[:, u, :].rearrange("p (b d) -> p b d", b=GB)
                    nc.vector.tensor_tensor(acc_b, acc_b, sb2_bc[:].unsqueeze(1).broadcast_to([P, GB, D]), ALU.add).then_inc(acc_init, 1)
                    dve.wait_ge(acc_init, j + 1)
                    for e in range(E + 1):
                        dve.wait_ge(l2_done, j * NCH + (CS + e * CR))
                        if e:
                            dve.wait_ge(acc_done, j * (E + 1) + e)
                        for b in range(GB):
                            a = acc[:, u, b * D:(b + 1) * D]
                            y_e = psum[:, 2 + e % 2, b * D:(b + 1) * D]
                            if e == 0:
                                ins = nc.vector.tensor_tensor(a, y_e, a, ALU.add)
                            else:
                                ins = nc.vector.scalar_tensor_tensor(a, y_e, gated_g[:, u, b, e - 1:e], a, ALU.mult, ALU.add)
                        ins.then_inc(acc_done, 1)
                    dve.wait_ge(acc_done, (j + 1) * (E + 1))
                    nc.vector.scalar_tensor_tensor(acc[:, u, :], acc[:, u, :], tanh_g[:, 1:2],
                                                   x_all[:, bass.ds(j * GB, GB), :].rearrange("p a d -> p (a d)"),
                                                   ALU.mult, ALU.add).then_inc(y_ready, 1)

        @block.tensor
        def _(pe):
            def front(i, gi, j):
                g = i * 2 + gi
                u = gi % 2
                ps = f_ps[j % 2]
                if not isinstance(g, int) or g * NF + j >= 2:
                    pe.wait_ge(front_out, g * NF + (j - 1))
                if j == 0:
                    pe.wait_ge(xn_ready, g + 1)
                    for b in range(GB):
                        ins = nc.tensor.transpose(ps[:, b * S:(b + 1) * S], xn[:, b, :], ident_sb[:])
                elif j < 5:
                    if j == 1:
                        pe.wait_ge(x_in, (g + 1) * 32)
                    ins = nc.tensor.matmul(ps[0:KS, 0:GB * KP], w_k3[:, j - 1, :], ctx_buf[:, u, :], start=True, stop=True)
                elif j < 9:
                    if j == 5:
                        pe.wait_ge(front_out, g * NF + 1)
                    ins = nc.tensor.matmul(ps[0:KS, :], w_q3[:, j - 5, :], xnT[:], start=True, stop=True)
                else:
                    for b in range(GB):
                        ins = nc.tensor.matmul(ps[0:KV, b * P:(b + 1) * P], ctx_buf[:, u, b * KP:b * KP + KV], w_vT[:],
                                               start=True, stop=True)
                ins.then_inc(front_done, 1)

            def scores(i, o, g):
                n = i * BODY + o
                u, b = o // GB % 2, o % GB
                if b == 0 and g == 0:
                    pe.wait_ge(k_heads_ready, i * 2 + (o // GB + 1))
                    pe.wait_ge(front_out, (i * 2 + o // GB) * NF + 9)
                if o >= 1 or g >= 2:
                    pe.wait_ge(max_done, n * 4 + (g - 1))
                rhs = k_heads[0:KS, u, g, :, b * KP:(b + 1) * KP]
                nc.tensor.matmul(s_ps[g % 2][:, 0:HQ * KP].rearrange("q (h k) -> q h k", h=HQ),
                                 q_stack[0:KS, u, g, b * S:(b + 1) * S], rhs, start=True, stop=True).then_inc(s_done, 1)

            def turn_max(i, o):
                n = i * BODY + o
                pe.wait_ge(max_done, n * 4 + 4)
                if o >= 3:
                    pe.wait_ge(x1_done, n - 2)
                for g in range(HG):
                    ins = nc.tensor.matmul(m_ps[0:KS + HQ, g * S:(g + 1) * S], max_cols[:, o % 2, g, :], ident_r[:],
                                           start=True, stop=True)
                ins.then_inc(mT_done, 1)

            def scores_t(i, o, g):
                n = i * BODY + o
                u, b = o // GB % 2, o % GB
                if g == 0:
                    pe.wait_ge(m_ready, n + 1)
                if o >= 1 or g >= 2:
                    pe.wait_ge(exp_done, n * 4 + (g - 1))
                for hh in range(HQ):
                    ins = nc.tensor.matmul(st_ps[g % 2][0:KV, hh * S:(hh + 1) * S], k_heads[:, u, g, hh, b * KP:b * KP + KV],
                                           q_stack[:, u, g, b * S:(b + 1) * S], start=True, stop=True)
                ins.then_inc(st_done, 1)

            def values(i, o, p):
                n = i * BODY + o
                if p == 0:
                    pe.wait_ge(exp_done, n * 4 + 4)
                    pe.wait_ge(v_den_ready, n + 1)
                    if o >= 1:
                        pe.wait_ge(on_ready, n)
                for h in range(HH):
                    ins = nc.tensor.matmul(o_ps[p], v_den[:, o % 2, p, h * P:(h + 1) * P],
                                           probs[:, o % 2, (p * HH + h) * S:(p * HH + h + 1) * S],
                                           start=(h == 0), stop=(h == HH - 1))
                ins.then_inc(av_done, 1)

            def project(i, o):
                n = i * BODY + o
                pe.wait_ge(on_ready, n + 1)
                if below(i, o + 2, B):
                    pe.wait_ge(m_ready, n + 3)
                else:
                    pe.wait_ge(x1_done, n)
                nc.tensor.matmul(y_ps, onT[:], w_oT[:], start=True, stop=True).then_inc(wo_done, 1)

            pe.wait_ge(w_in, 6 * 16)
            pe.wait_ge(zeroed, 2)
            pe.wait_ge(id_ready, 1)
            pe.wait_ge(fill_zeroed, 2)
            for j in range(NF):
                front(0, 0, j)
            for g in range(HG):
                scores(0, 0, g)

            def slot(i, o):
                fr = PIECES[o % GB] if below(i, o, B - GB) else ()
                if below(i, o + 1, B):
                    scores(i, o + 1, 0)
                    scores(i, o + 1, 1)
                if below(i, o, B):
                    turn_max(i, o)
                    scores_t(i, o, 0)
                    scores_t(i, o, 1)
                if o >= 2:
                    project(i, o - 2)
                for j in fr[0:1]:
                    front(i, o // GB + 1, j)
                if o >= 1 and below(i, o, B + 1):
                    values(i, o - 1, 0)
                if below(i, o, B):
                    scores_t(i, o, 2)
                    scores_t(i, o, 3)
                for j in fr[1:2]:
                    front(i, o // GB + 1, j)
                if below(i, o + 1, B):
                    scores(i, o + 1, 2)
                    scores(i, o + 1, 3)
                if o >= 1 and below(i, o, B + 1):
                    values(i, o - 1, 1)
                for j in fr[2:]:
                    front(i, o // GB + 1, j)

            walk(pe, slot)
            pe.wait_ge(moe_in, 10 * 16)
            with pe.Fori(0, NG) as j:
                pe.wait_ge(xn2_ready, j + 1)
                pe.wait_ge(x2T_out, j)
                for b in range(GB):
                    ins = nc.tensor.transpose(psum[:, 0, b * S:(b + 1) * S], xn[:, b, :], ident_sb[:])
                ins.then_inc(x2T_done, 1)
                pe.wait_ge(x2T_out, j + 1)
                pe.wait_ge(lg_out, j)
                for b in range(GB):
                    ins = nc.tensor.matmul(psum[:, 1, b * E:(b + 1) * E], xn2T_buf[:, b * S:(b + 1) * S], gw_sb[:],
                                           start=True, stop=True)
                ins.then_inc(lg_done, 1)
            pe.wait_ge(x2T_kept, NG)
            pe.wait_ge(gated_ready, 1)
            def gate_bias(j, u):
                pe.wait_ge(gates_in, j + 1)
                pe.wait_ge(gT_out, j)
                for b in range(GB):
                    ins = nc.tensor.transpose(psum[0:E, 4, b * S:(b + 1) * S], gated_g[:, u, b, :], ident_sb[:])
                ins.then_inc(gT_done, 1)
                pe.wait_ge(gT_out, j + 1)
                pe.wait_ge(acc_init, j)
                for b in range(GB):
                    ins = nc.tensor.matmul(psum[:, 5, b * D:(b + 1) * D], gatedT[:, b * S:(b + 1) * S], b2row[:],
                                           start=True, stop=True)
                ins.then_inc(bias_done, 1)

            def layer1(j, c):
                if c >= 2:
                    pe.wait_ge(gelu_done, j * NCH + (c - 1))
                else:
                    pe.wait_ge(gelu_done, j * NCH)
                nc.tensor.matmul(psum[:, c % 2, :], w1[:, c, :], xn2T[:, bass.ds(j * GT, GT)],
                                 start=True, stop=True).then_inc(l1_done, 1)

            def layer2(j, c):
                e, first, last = (0, c == 0, c == CS - 1) if c < CS else \
                    ((c - CS) // CR + 1, (c - CS) % CR == 0, (c - CS) % CR == CR - 1)
                pe.wait_ge(gelu_done, j * NCH + (c + 1))
                if first and e >= 2:
                    pe.wait_ge(acc_done, j * (E + 1) + (e - 1))
                elif first:
                    pe.wait_ge(acc_done, j * (E + 1))
                for b in range(GB):
                    ins = nc.tensor.matmul(psum[:, 2 + e % 2, b * D:(b + 1) * D], hid[:, c % 2, b * S:(b + 1) * S], w2[:, c, :],
                                           start=first and b == 0, stop=last, skip_group_check=True)
                ins.then_inc(l2_done, 1)

            with pe.Fori(0, NG // 2) as jj:
                for u in range(2):
                    j = jj * 2 + u
                    layer1(j, 0)
                    gate_bias(j, u)
                    for c in range(NCH):
                        if c + 1 < NCH:
                            layer1(j, c + 1)
                        layer2(j, c)


_INS = ["x", "ctxT", "g_xattn", "g_ffn", "wqT3", "wkT3", "wvT", "woT", "w1_chunks", "b1_cols", "w2_chunks", "sb2",
        "rb2", "gW", "gb", "ident", "head_of_row", "rev_idx"]


def kernel(**inputs):
    import numpy as np
    import concourse.bacc as bacc
    from concourse.bass_utils import run_bass_kernel_spmd

    data = {k.replace("L0_xattn_", "").replace("L0_ffn_", ""): np.asarray(v) for k, v in inputs.items()}
    ctx = data.pop("ctx_1024")
    ctx = np.concatenate([ctx, ctx[:, -1:]], axis=1)
    data["ctxT"] = ctx.transpose(2, 0, 1).reshape(ctx.shape[2], -1)
    for n in "qkvo":
        data[f"w{n}T"] = data.pop(f"w_{n}").T
    for n in "qk":
        w = data[f"w{n}T"]
        data[f"w{n}T3"] = np.broadcast_to(w.reshape(len(w), 4, 1, 32), (len(w), 4, 3, 32)).reshape(len(w), 4, 96)
    d = data["sW1"].shape[1]
    data["w1_chunks"] = np.concatenate(
        [w.reshape(len(w), d, -1, P).transpose(1, 0, 2, 3).reshape(d, -1, P) for w in (data["sW1"], data["rW1"])], axis=1)
    data["w2_chunks"] = np.concatenate([w.reshape(-1, P, d).transpose(1, 0, 2) for w in (data["sW2"], data["rW2"])], axis=1)
    data["b1_cols"] = np.concatenate([b.reshape(-1, P) for b in (data["sb1"], data["rb1"])]).T
    rows = np.arange(P)
    heads = np.where(rows < 96, rows // 8 % 4, rows - 96)
    data["ident"] = np.eye(P, dtype=np.float32)
    data["head_of_row"] = (heads[:, None] == np.arange(4)[None]).astype(np.float32)
    experts = data["gW"].shape[1]
    data["rev_idx"] = np.broadcast_to(experts - np.arange(experts, dtype=np.float32), (P, experts))

    nc = bacc.Bacc("TRN2", target_bir_lowering=False, num_devices=1)
    arrays, args = {}, []
    for name in _INS:
        a = np.ascontiguousarray(data[name])
        arrays[f"in_{name}"] = a
        args.append(nc.dram_tensor(f"in_{name}", a.shape, mybir.dt.from_np(a.dtype), kind="ExternalInput").ap())
    shape = data["x"].shape
    args.append(nc.dram_tensor("out_0", shape, F32, kind="ExternalOutput").ap())
    flamingo_kernel(nc, *args)
    r = run_bass_kernel_spmd(nc, [arrays], core_ids=[0])
    return r.results[0]["out_0"]
```

```python
import math
from contextlib import ExitStack

import concourse.bass as bass
from concourse import mybir

P = 128
F32 = mybir.dt.float32
F32R = mybir.dt.float32r
ALU = mybir.AluOpType
ACT = mybir.ActivationFunctionType
AX = mybir.AxisListType
EPS = 1e-5


def flamingo_kernel(nc, x, ctxT, g_xattn, g_ffn, wqT, wkT, wvT, woT, w_chunks, b1_cols, b2_rows,
                    gW, gb, ident, head_of_row, gate_rows, rev_idx, out):
    B, S, D = x.shape
    KP = ctxT.shape[1] // B
    KV = KP - 1
    H, DK = 16, 8
    HQ = P // DK // 4
    GB = 4
    NG = B // GB
    GT = GB * S
    E = gW.shape[1]
    NCH = w_chunks.shape[2]
    CR, CS = 2, 4
    AHEAD = 3
    ROUTE = 27
    assert NCH == CS + E * CR
    SCALE = float(DK) ** -0.5
    BODY = 2 * GB
    LEAD = 3
    HG = H // HQ
    KS = 3 * HQ * DK
    HH = H // 2
    VB = HH * (P + DK) + P // 2
    NF = 4
    PIECES = ((0, None, None), (1, None, 2), (None, None, None), (None, 3, None))
    PARTS = (((0, 1, 2, 3), (), ()), ((), (), (4,)), ((5,), (6,), (7,)), ((), (), ()))
    GR = HQ * DK

    with ExitStack() as ctx:
        def sb(name, shape, dt=F32):
            return ctx.enter_context(nc.sbuf_tensor(name, shape, dt))

        def sem(name):
            return ctx.enter_context(nc.semaphore(name))

        x_all = sb("x_all", [P, B, D])
        ctx_buf = sb("ctx_buf", [P, 2, GB * KP])
        w_qT, w_kT, w_vT, w_oT = (sb(n, [P, P]) for n in ("w_qT", "w_kT", "w_vT", "w_oT"))
        w_lo = sb("w_lo", [P, 2, NCH, P], F32R)
        b1c = sb("b1c", [P, NCH])
        b2 = sb("b2_rows", [P, D])
        b2_parts = sb("b2_parts", [P, 2, D], F32R)
        gw_sb = sb("gw_sb", [P, E])
        gb_bc = sb("gb_bc", [P, E])
        ident_sb = sb("ident_sb", [P, P])
        head_mask = sb("head_mask", [P, HQ])
        gate_pick = sb("gate_pick", [P, E + 1])
        gate_pick_r = sb("gate_pick_r", [P, E + 1], F32R)
        rev_sb = sb("rev_sb", [P, E])
        half_pow = sb("half_pow", [P, B])
        euler = sb("euler", [P, GB, E])
        gates = sb("gates", [P, 2])
        tanh_g = sb("tanh_g", [P, 2])
        stats = sb("stats", [P, GB, 6])
        mv1 = sb("mv1", [P, GB, 2])
        var1 = sb("var1", [P, GB])
        rstd1 = sb("rstd1", [P, GB])
        xn = sb("xn", [P, GB, D])
        xnT = sb("xnT", [P, GT])
        q_stack = sb("q_stack", [P, 2, HG, GT], F32R)
        k_stack = sb("k_stack", [P, HG, GB * KP])
        k_heads = sb("k_heads", [P, 2, HG, HQ, GB * KP], F32R)
        max_cols = sb("max_cols", [P, 2, P], F32R)
        ident_r = sb("ident_r", [P, P], F32R)
        v_all = sb("v_all", [P, 2, GT])
        v_den = sb("v_den", [P, 2, 2, VB])
        probs = sb("probs", [P, 2, H * S])
        den = sb("den", [P, S])
        r_den = sb("r_den", [P, S])
        onT = sb("onT", [P, 2, S])
        stats2 = sb("stats2", [P, B, 6])
        mv2 = sb("mv2", [P, B, 2])
        var2 = sb("var2", [P, B])
        rstd2 = sb("rstd2", [P, B])
        gw_parts = sb("gw_parts", [P, 2, E], F32R)
        x2_hi, x2_lo = (sb(n, [P, 2, GT], F32R) for n in ("x2_hi", "x2_lo"))
        logits, weights, left, pick, pick2 = (sb(n, [P, GB, E]) for n in ("logits", "weights", "left", "pick", "pick2"))
        top, total, inverse, place = (sb(n, [P, GB]) for n in ("top", "total", "inverse", "place"))
        gates_f = sb("gates_f", [P, GB, E])
        gate_cols = sb("gate_cols", [P, 2, GB, 32 + E + 1], F32R)
        gatesT = sb("gatesT", [P, 2, GT], F32R)
        lgT = xnT[0:E, :]
        w_hi = k_heads[:].rearrange("p u g h k -> p (u g h k)")[:, 0:2 * NCH * P].rearrange("p (m c f) -> p m c f", m=2, c=NCH)
        w_raw = [buf[:, r * 4 * P:(r + 1) * 4 * P].rearrange("p (m c f) -> p m c f", m=2, c=2)
                 for buf in (k_stack[:].rearrange("p g k -> p (g k)"), v_all[:].rearrange("p u t -> p (u t)")) for r in range(2)]
        v_flat = v_den[:].rearrange("p r q c -> p (r q c)")
        hid_gated = [v_flat[:, r * GT:(r + 1) * GT] for r in range(4)]
        hid = probs[:, 0, 0:2 * GT].rearrange("p (r t) -> p r t", r=2)
        out_buf = probs[:, 1, 0:2 * GT].rearrange("p (r t) -> p r t", r=2)
        yT_sb = probs[:, 1, 2 * GT:3 * GT]
        h_parts = sb("h_parts", [P, 2, 4, GT], F32R)
        h_hi, h_lo = h_parts[:, 0], h_parts[:, 1]

        psum = ctx.enter_context(nc.psum_tensor("psum", [P, 8, 512], F32))
        s_ps = [psum[:, 0, :], psum[:, 1, :]]
        st_ps = [psum[:, 2, :], psum[:, 3, :]]
        m_ps = psum[:, 4, :]
        y_ps = psum[:, 4, 0:D]
        f_ps = psum[:, 5, :]
        o_ps = [[psum[:, 6 + r, p * S:(p + 1) * S] for p in range(2)] for r in range(2)]

        passed = sem("passed")
        w_in = sem("w_in")
        x_in = sem("x_in")
        moe_in = sem("moe_in")
        zeroed = sem("zeroed")
        fill_zeroed = sem("fill_zeroed")
        tanh_done = sem("tanh_done")
        ln1_var = sem("ln1_var")
        ln1_rstd = sem("ln1_rstd")
        xn_ready = sem("xn_ready")
        front_done = sem("front_done")
        parts_out = sem("parts_out")
        xT_out = sem("xT_out")
        v_out = sem("v_out")
        front_hi = sem("front_hi")
        k_heads_ready = sem("k_heads_ready")
        k_half_ready = sem("k_half_ready")
        v_den_ready = sem("v_den_ready")
        id_ready = sem("id_ready")
        s_done = sem("s_done")
        max_done = sem("max_done")
        mT_done = sem("mT_done")
        m_ready = sem("m_ready")
        st_done = sem("st_done")
        exp_done = sem("exp_done")
        av_done = sem("av_done")
        den_out = sem("den_out")
        rden_done = sem("rden_done")
        on_ready = sem("on_ready")
        wo_done = sem("wo_done")
        x1_done = sem("x1_done")

        ln2_var = sem("ln2_var")
        ln2_rstd = sem("ln2_rstd")
        xn2_ready = sem("xn2_ready")
        lgT_done = sem("lgT_done")
        lgT_out = sem("lgT_out")
        lg_done = sem("lg_done")
        soft_exp = sem("soft_exp")
        route_step = sem("route_step")
        stats1_done = sem("stats1_done")
        mv1_done = sem("mv1_done")
        stats2_done = sem("stats2_done")
        mv2_done = sem("mv2_done")
        w_raw_in = [sem(f"w_raw{r}_in") for r in range(4)]
        w_split = sem("w_split")
        b2_split = sem("b2_split")
        gates_fill = sem("gates_fill")
        x2T_done = sem("x2T_done")
        x2_hi_ready = sem("x2_hi_ready")
        x2_lo_ready = sem("x2_lo_ready")
        gT_done = sem("gT_done")
        gT_out = sem("gT_out")
        spread_done = sem("spread_done")
        l1_done = sem("l1_done")
        gelu_done = sem("gelu_done")
        h_gated = sem("h_gated")
        h_hi_ready = sem("h_hi_ready")
        h_lo_ready = sem("h_lo_ready")
        l2_done = sem("l2_done")
        yT_out = sem("yT_out")
        y_turned = sem("y_turned")
        y_ready = sem("y_ready")
        y_out = sem("y_out")
        out_free = sem("out_free")

        block = ctx.enter_context(nc.Block())

        def walk(eng, slot):
            for o in range(LEAD):
                slot(0, o)
            with eng.Fori(0, NG // 2 - 1) as i:
                for o in range(LEAD, LEAD + BODY):
                    slot(i, o)
            for o in range(LEAD, LEAD + BODY):
                slot(NG // 2 - 1, o)

        def front_bank(g, j):
            return psum[:, 5 + j % 3, :] if isinstance(g, int) and g == 0 else f_ps

        def prep_bank(i, o, bank):
            return 5 if isinstance(i, int) and i * 2 + o == 0 else bank

        def below(i, o, limit):
            return not isinstance(i, int) or i * BODY + o < limit

        def walk_groups(eng, group):
            group(0, 0)
            with eng.Fori(0, NG // 2 - 1) as i:
                for o in (1, 2):
                    group(i, o)
            group(NG // 2 - 1, 1)

        @block.sync
        def _(sp):
            def load_group(i, u):
                g = i * 2 + u
                if not isinstance(g, int) or g > 0:
                    sp.wait_ge(x_in, g * 32)
                    sp.sem_inc(passed, 1)
                if not isinstance(i, int) or i > 0:
                    sp.wait_ge(v_out, i * 2 + (u - 1))
                    sp.sem_inc(passed, 1)
                sp.dma_start(x_all[:, bass.ds(g * GB, GB), :],
                             x[bass.ds(g * GB, GB), :, :].rearrange("b t d -> t b d")).then_inc(x_in, 16)
                sp.dma_start(ctx_buf[:, u, :], ctxT[:, bass.ds(g * (GB * KP), GB * KP)]).then_inc(x_in, 16)

            load_group(0, 0)
            for dst, src in ((w_kT, wkT), (ident_sb, ident), (w_qT, wqT), (w_vT, wvT), (head_mask, head_of_row), (w_oT, woT)):
                sp.dma_start(dst[:], src).then_inc(w_in, 16)
            load_group(0, 1)
            sp.wait_ge(fill_zeroed, 2)
            for dst, src in ((gates[:, 0:1], g_xattn.rearrange("(a b) -> a b", a=1).partition_broadcast(P)),
                             (gates[:, 1:2], g_ffn.rearrange("(a b) -> a b", a=1).partition_broadcast(P)),
                             (gb_bc[:], gb.rearrange("(a e) -> a e", a=1).partition_broadcast(P)),
                             (rev_sb[:], rev_idx), (gw_sb[:], gW), (gate_pick[:], gate_rows),
                             (b2[0:E + 1, :], b2_rows), (b2[32:32 + E + 1, :], b2_rows), (b1c[:], b1_cols)):
                sp.dma_start(dst, src).then_inc(moe_in, 16)
            with sp.Fori(1, NG // 2) as i:
                for u in range(2):
                    load_group(i, u)
            sp.wait_ge(k_heads_ready, NG)
            sp.wait_ge(v_den_ready, B)

            def load_weights(i, r):
                p = i * 4 + r
                if not isinstance(i, int) or i > 0:
                    sp.wait_ge(w_split, (i * 4 + (r - 3)) * 2)
                    sp.sem_inc(passed, 1)
                sp.dma_start(w_raw[r], w_chunks[:, :, bass.ds(p * 2, 2), :]).then_inc(w_raw_in[r], 16)

            for r in range(4):
                load_weights(0, r)
            with sp.Fori(1, NCH // 8) as i:
                for r in range(4):
                    load_weights(i, r)
            load_weights(NCH // 8, 0)

            def group(i, o):
                j = i * 2 + o
                sp.wait_ge(y_ready, j + 1)
                sp.sem_inc(passed, 1)
                sp.dma_start(out[bass.ds(j * GB, GB), :, :].rearrange("b t d -> t b d"),
                             out_buf[:, o % 2, :].rearrange("p (b d) -> p b d", b=GB)).then_inc(y_out, 16)
                sp.wait_ge(y_out, (j + 1) * 16)
                sp.sem_inc(out_free, 1)

            sp.sem_inc(out_free, 2)
            walk_groups(sp, group)

        @block.gpsimd
        def _(pool):
            pool.memset(half_pow[:], -0.5)
            pool.memset(euler[:], math.e)
            pool.memset(max_cols[:].bitcast(F32), 0.0)
            pool.memset(probs[:], 0.0)
            pool.memset(k_stack[:], -1.0).then_inc(zeroed, 1)

            def rstd(g):
                pool.wait_ge(ln1_var, g + 1)
                nc.gpsimd.tensor_tensor(rstd1[:], var1[:], half_pow[:, 0:GB], ALU.pow).then_inc(ln1_rstd, 1)

            def expand_k(g, u):
                pool.wait_ge(parts_out, (g * 2 + 1) * HG)
                pool.sem_inc(passed, 1)
                for hh in range(HQ // 2 if isinstance(g, int) and g == 0 else HQ):
                    ins = nc.gpsimd.tensor_scalar(k_heads[:, u, :, hh, :], k_stack[:], head_mask[:, hh:hh + 1], 1.0, ALU.mult, ALU.mult)
                ins.then_inc(k_heads_ready, 1)

            def place_v(i, o):
                n = i * BODY + o
                u, b = o // GB % 2, o % GB
                pool.wait_ge(v_out, i * 2 + (o // GB + 1))
                pool.sem_inc(passed, 1)
                if o >= 2:
                    pool.wait_ge(av_done, n * 2 - 2)
                    pool.sem_inc(passed, 1)
                for p in range(2):
                    dst = v_den[0:KV, o % 2, p, p * 64:p * 64 + HH * (P + DK)].rearrange("k (h c) -> k h c", h=HH)[:, :, 0:DK]
                    src = v_all[0:KV, u, b * P + p * 64:b * P + p * 64 + 64].rearrange("k (h c) -> k h c", h=HH)
                    ins = nc.gpsimd.tensor_copy(dst, src)
                ins.then_inc(v_den_ready, 1)

            pool.wait_ge(zeroed, 1)
            rstd(0)
            pool.wait_ge(w_in, 6 * 16)
            expand_k(0, 0)
            pool.memset(v_den[:], 0.0).then_inc(zeroed, 1)
            pool.wait_ge(zeroed, 2)
            for r in range(2):
                for p in range(2):
                    ones = v_den[:, r, p, (1 - p) * 64:(1 - p) * 64 + HH * (P + DK)].rearrange("k (h c) -> k h c", h=HH)[:, :, 0:DK]
                    ins = pool.memset(ones, 1.0)
            ins.then_inc(zeroed, 1)
            pool.wait_ge(zeroed, 3)
            rstd(1)

            def slot(i, o):
                if below(i, o, B):
                    place_v(i, o)
                if o % GB == 1 and below(i, o, B - GB):
                    expand_k(i * 2 + o // GB + 1, (o // GB + 1) % 2)
                if o % GB == 3 and below(i, o, B - 2 * GB):
                    rstd(i * 2 + o // GB + 2)

            walk(pool, slot)
            def rstd2_of(k, cols):
                pool.wait_ge(ln2_var, k + 1)
                nc.gpsimd.tensor_tensor(rstd2[:, cols], var2[:, cols], half_pow[:, cols], ALU.pow).then_inc(ln2_rstd, 1)

            rstd2_of(0, slice(0, GB))

            pool.wait_ge(st_done, B * HG)
            for p in range(NCH // 2):
                if p == 4:
                    rstd2_of(1, slice(GB, B - GB))
                    rstd2_of(2, slice(B - GB, B))
                chunks = slice(p * 2, p * 2 + 2)
                pool.wait_ge(w_raw_in[p % 4], (p // 4 + 1) * 16)
                nc.gpsimd.tensor_scalar(w_hi[:, :, chunks, :], w_raw[p % 4], 1.0, 1.0, ALU.mult, ALU.mult).then_inc(w_split, 1)
                pool.wait_ge(w_split, p * 2 + 1)
                nc.gpsimd.tensor_tensor(w_lo[:, :, chunks, :], w_raw[p % 4], w_hi[:, :, chunks, :].bitcast(F32), ALU.subtract).then_inc(w_split, 1)

            def group(i, o):
                j = i * 2 + o
                if not isinstance(j, int) or j < NG - 1:
                    pool.wait_ge(route_step, (j + 1) * ROUTE + 3)
                    pool.sem_inc(passed, 1)
                    nc.gpsimd.tensor_tensor(weights[:], euler[:], logits[:], ALU.pow).then_inc(soft_exp, 1)

            walk_groups(pool, group)

        @block.scalar
        def _(act):
            def leading(i, gi, unit):
                g = i * 2 + gi
                u = gi % 2
                j, hg = unit // HG * 2, unit % HG
                src = front_bank(g, j)[hg * GR:(hg + 1) * GR]
                if hg == 0:
                    act.wait_ge(front_done, g * NF + (j + 1))
                for r in (1, 0) if j == 0 else (2, 0):
                    if j == 0:
                        ins = nc.scalar.activation(k_stack[r * GR:(r + 1) * GR, hg, :].bitcast(F32R), src[:, 0:GB * KP], ACT.Copy)
                    else:
                        ins = nc.scalar.activation(q_stack[r * GR:(r + 1) * GR, u, hg, :], src, ACT.Copy)
                ins.then_inc(front_hi, 1)

            def denominators(i, o):
                n = i * BODY + o
                act.wait_ge(av_done, n * 2 + 2)
                if o >= 1:
                    act.wait_ge(rden_done, n)
                lower, upper = o_ps[o % 2]
                nc.scalar.activation(den[0:64, :], lower[64:128, :], ACT.Copy)
                nc.scalar.activation(den[64:128, :], upper[0:64, :], ACT.Copy).then_inc(den_out, 1)

            act.wait_ge(w_in, 6 * 16)
            nc.scalar.activation(ident_r[:], ident_sb[:], ACT.Copy).then_inc(id_ready, 1)
            act.wait_ge(zeroed, 1)
            for unit in range(2 * HG):
                leading(0, 0, unit)
            act.wait_ge(moe_in, 9 * 16)
            nc.scalar.activation(tanh_g[:], gates[:], ACT.Tanh).then_inc(tanh_done, 1)
            act.wait_ge(fill_zeroed, 2)

            def max_rows(i, o):
                u, b = o // GB % 2, o % GB
                act.wait_ge(mT_done, i * BODY + (o + 1))
                for g in range(HG):
                    ins = nc.scalar.activation(q_stack[KS:KS + HQ, u, g, b * S:(b + 1) * S], m_ps[g * GR:g * GR + HQ, 0:S], ACT.Copy)
                ins.then_inc(m_ready, 1)

            def x2_leading(i, o):
                act.wait_ge(x2T_done, i * 2 + (o + 1))
                nc.scalar.activation(x2_hi[:, o % 2, :], psum[:, prep_bank(i, o, 6), :], ACT.Copy).then_inc(x2_hi_ready, 1)

            def exps(i, o, g):
                n = i * BODY + o
                act.wait_ge(st_done, n * 4 + (g + 1))
                if g == 0 and o >= 2:
                    act.wait_ge(av_done, n * 2 - 2)
                nc.scalar.activation(probs[0:KV, o % 2, g * 512:(g + 1) * 512], st_ps[g % 2][0:KV, :],
                                     ACT.Exp, scale=SCALE).then_inc(exp_done, 1)

            def logits_turned_out(i, o):
                act.wait_ge(lgT_done, i * 2 + (o + 1))
                nc.scalar.activation(lgT, psum[0:E, prep_bank(i, o, 7), :], ACT.Copy).then_inc(lgT_out, 1)

            def slot(i, o):
                parts = PARTS[o % GB] if below(i, o, B - GB) else ((), (), ())
                if o >= 2 and below(i, o, B + 2):
                    denominators(i, o - 2)
                if below(i, o, B):
                    exps(i, o, 0)
                    exps(i, o, 1)
                for unit in parts[0]:
                    leading(i, o // GB + 1, unit)
                if below(i, o, B):
                    exps(i, o, 2)
                    exps(i, o, 3)
                for unit in parts[1]:
                    leading(i, o // GB + 1, unit)
                if below(i, o + 1, B):
                    max_rows(i, o + 1)
                for unit in parts[2]:
                    leading(i, o // GB + 1, unit)
                if not below(i, o, B):
                    if i * BODY + o == B:
                        x2_leading(0, 0)
                    elif i * BODY + o == B + 1:
                        logits_turned_out(0, 0)

            max_rows(0, 0)
            walk(act, slot)
            def exp_logits(i, o):
                act.wait_ge(route_step, (i * 2 + o) * ROUTE + 3)
                nc.scalar.activation(weights[:], logits[:], ACT.Exp).then_inc(soft_exp, 1)

            def gelu(i, o, c):
                m = (i * 2 + o) * NCH + c
                act.wait_ge(l1_done, m + 1)
                if c < CS:
                    dst = hid_gated[(2 * o + c) % 4]
                    if isinstance(m, int) and m < 4:
                        act.wait_ge(av_done, B * 2)
                    else:
                        act.wait_ge(h_lo_ready, m - 3)
                else:
                    dst = hid[:, c % 2, :]
                    before = (i * 2 + o) * (NCH - CS) + (c - CS - 1)
                    if not isinstance(before, int) or before > 0:
                        act.wait_ge(h_gated, before)
                nc.scalar.activation(dst, psum[:, c % 2, :], ACT.Gelu, bias=b1c[:, c:c + 1]).then_inc(gelu_done, 1)

            def leading_h(i, o, c):
                m = (i * 2 + o) * NCH + c
                if c < CS:
                    act.wait_ge(gelu_done, m + 1)
                else:
                    act.wait_ge(h_gated, (i * 2 + o) * (NCH - CS) + (c - CS + 1))
                if not isinstance(m, int) or m >= 4:
                    act.wait_ge(l2_done, m - 3)
                nc.scalar.activation(h_hi[:, (2 * o + c) % 4, :], hid_gated[(2 * o + c) % 4], ACT.Copy).then_inc(h_hi_ready, 1)

            def gates_out(i, o):
                act.wait_ge(gT_done, i * 2 + (o + 1))
                nc.scalar.activation(gatesT[0:32 + E + 1, o % 2, :], psum[0:32 + E + 1, prep_bank(i, o, 7), :], ACT.Copy).then_inc(gT_out, 1)

            def group(i, o):
                last = isinstance(i, int) and i * 2 + o == NG - 1
                for c in range(NCH):
                    if c + 1 < NCH:
                        gelu(i, o, c + 1)
                    elif not last:
                        gelu(i, o + 1, 0)
                    leading_h(i, o, c)
                    if not last:
                        if c == 3:
                            x2_leading(i, o + 1)
                        if c == 7:
                            logits_turned_out(i, o + 1)
                        if c == 33:
                            gates_out(i, o + 1)
                    if isinstance(i, int) and i * 2 + o == 0 and c == 2:
                        gates_out(0, 0)

            exp_logits(0, 0)
            gelu(0, 0, 0)
            walk_groups(act, group)

        @block.vector
        def _(dve):
            def front_copy(i, gi, j):
                g = i * 2 + gi
                ps = front_bank(g, j)
                dve.wait_ge(front_done, g * NF + (j + 1))
                if j == 1:
                    nc.vector.tensor_copy(xnT[:], ps).then_inc(xT_out, 1)
                else:
                    nc.vector.tensor_copy(v_all[0:KV, gi % 2, :], ps[0:KV, :]).then_inc(v_out, 1)

            def trailing(i, gi, unit):
                g = i * 2 + gi
                u = gi % 2
                j, hg = unit // HG * 2, unit % HG
                src = front_bank(g, j)[hg * GR:(hg + 1) * GR]
                dve.wait_ge(front_hi, g * (2 * HG) + (unit + 1))
                if j == 0:
                    ins = nc.vector.tensor_tensor(k_stack[2 * GR:3 * GR, hg, :].bitcast(F32R), src[:, 0:GB * KP],
                                                  k_stack[0:GR, hg, :], ALU.subtract)
                else:
                    ins = nc.vector.tensor_tensor(q_stack[GR:2 * GR, u, hg, :], src,
                                                  q_stack[0:GR, u, hg, :].bitcast(F32), ALU.subtract)
                ins.then_inc(parts_out, 1)

            def ln1_stats(i, gi):
                g = i * 2 + gi
                dve.wait_ge(x_in, (g + 1) * 32)
                dve.sem_inc(passed, 1)
                for b in range(GB):
                    ins = nc.vector.bn_stats(stats[:, b, :], x_all[:, bass.ds(g * GB + b, 1), :].rearrange("p a d -> p (a d)"))
                ins.then_inc(stats1_done, 1)
                dve.wait_ge(stats1_done, g + 1)
                dve.sem_inc(passed, 1)
                for b in range(GB):
                    ins = nc.vector.bn_aggr(mv1[:, b, :], stats[:, b, :])
                ins.then_inc(mv1_done, 1)
                dve.wait_ge(mv1_done, g + 1)
                nc.vector.tensor_scalar(var1[:], mv1[:, :, 1:2].rearrange("p b a -> p (b a)"), EPS, None, ALU.add).then_inc(ln1_var, 1)

            def ln1_apply(i, gi):
                g = i * 2 + gi
                dve.wait_ge(ln1_rstd, g + 1)
                for b in range(GB):
                    ins = nc.vector.tensor_scalar(xn[:, b, :], x_all[:, bass.ds(g * GB + b, 1), :].rearrange("p a d -> p (a d)"),
                                                  mv1[:, b, 0:1], rstd1[:, b:b + 1], ALU.subtract, ALU.mult)
                ins.then_inc(xn_ready, 1)

            nc.vector.memset(q_stack[KS:P, :, :, :].bitcast(F32), 0.0).then_inc(fill_zeroed, 1)
            ln1_stats(0, 0)
            ln1_apply(0, 0)
            nc.vector.memset(b2[:], 0.0).then_inc(fill_zeroed, 1)
            dve.wait_ge(zeroed, 1)
            front_copy(0, 0, 1)
            for unit in range(HG):
                trailing(0, 0, unit)
            dve.wait_ge(parts_out, HG)
            dve.wait_ge(w_in, 6 * 16)
            for hh in range(HQ // 2, HQ):
                ins = nc.vector.tensor_scalar(k_heads[:, 0, :, hh, :], k_stack[:], head_mask[:, hh:hh + 1], 1.0, ALU.mult, ALU.mult)
            ins.then_inc(k_half_ready, 1)
            nc.vector.memset(gatesT[:].bitcast(F32), 0.0).then_inc(gates_fill, 1)
            nc.vector.memset(gate_cols[:].bitcast(F32), 0.0).then_inc(gates_fill, 1)
            dve.wait_ge(gates_fill, 2)
            nc.vector.memset(gate_cols[:, :, :, E:E + 1].bitcast(F32), 1.0).then_inc(gates_fill, 1)
            for unit in range(HG, 2 * HG):
                trailing(0, 0, unit)
            front_copy(0, 0, 3)
            ln1_stats(0, 1)

            def maxima(i, o, g):
                n = i * BODY + o
                if o >= 2 and g == 0:
                    dve.wait_ge(mT_done, n - 1)
                dve.wait_ge(s_done, n * 4 + (g + 1))
                nc.vector.tensor_reduce(max_cols[:, o % 2, g * GR:g * GR + HQ],
                                        s_ps[g % 2][:, 0:HQ * KP].rearrange("q (h k) -> q h k", h=HQ), AX.X, ALU.max).then_inc(max_done, 1)

            def tile(n):
                return x_all[:, bass.ds(n, 1), :].rearrange("p a d -> p (a d)")

            def residual(i, o):
                n = i * BODY + o
                dve.wait_ge(wo_done, n + 1)
                nc.vector.scalar_tensor_tensor(tile(n), y_ps, tanh_g[:, 0:1], tile(n), ALU.mult, ALU.add).then_inc(x1_done, 1)

            def residual_stats(i, o):
                n = i * BODY + o
                dve.wait_ge(x1_done, n + 1)
                dve.sem_inc(passed, 1)
                nc.vector.bn_stats(stats2[:, bass.ds(n, 1), :].rearrange("p a d -> p (a d)"), tile(n)).then_inc(stats2_done, 1)

            def invert(i, o):
                dve.wait_ge(den_out, i * BODY + (o + 1))
                nc.vector.reciprocal(r_den[:], den[:]).then_inc(rden_done, 1)

            def normalise(i, o):
                n = i * BODY + o
                lower, upper = o_ps[o % 2]
                dve.wait_ge(rden_done, n + 1)
                if o >= 2:
                    dve.wait_ge(wo_done, n - 1)
                nc.vector.tensor_tensor(onT[0:64, o % 2, :], lower[0:64, :], r_den[0:64, :], ALU.mult)
                nc.vector.tensor_tensor(onT[64:128, o % 2, :], upper[64:128, :], r_den[64:128, :], ALU.mult).then_inc(on_ready, 1)

            for g in range(HG):
                maxima(0, 0, g)
            dve.wait_ge(tanh_done, 1)

            def split_small():
                dve.wait_ge(moe_in, 9 * 16)
                nc.vector.tensor_copy(gate_pick_r[:], gate_pick[:])
                nc.vector.tensor_copy(gw_parts[:, 0, :], gw_sb[:]).then_inc(b2_split, 1)
                nc.vector.tensor_copy(b2_parts[:, 0, :], b2[:]).then_inc(b2_split, 1)
                dve.wait_ge(b2_split, 2)
                nc.vector.tensor_tensor(gw_parts[:, 1, :], gw_sb[:], gw_parts[:, 0, :].bitcast(F32), ALU.subtract).then_inc(b2_split, 1)
                nc.vector.tensor_tensor(b2_parts[:, 1, :], b2[:], b2_parts[:, 0, :].bitcast(F32), ALU.subtract).then_inc(b2_split, 1)

            def ln2_stats(k, first, end):
                dve.wait_ge(stats2_done, end)
                for n in range(first, end):
                    ins = nc.vector.bn_aggr(mv2[:, n, :], stats2[:, n, :])
                ins.then_inc(mv2_done, 1)
                dve.wait_ge(mv2_done, k + 1)
                nc.vector.tensor_scalar(var2[:, first:end], mv2[:, first:end, 1:2].rearrange("p b a -> p (b a)"), EPS, None,
                                        ALU.add).then_inc(ln2_var, 1)

            def normalise_group(i, o):
                j = i * 2 + o
                if isinstance(j, int) and j < 2:
                    dve.wait_ge(ln2_rstd, 2 * j + 1)
                if not isinstance(j, int) or j > 0:
                    dve.wait_ge(x2T_done, j)
                    dve.sem_inc(passed, 1)
                for b in range(GB):
                    t = j * GB + b
                    ins = nc.vector.tensor_scalar(xn[:, b, :], x_all[:, bass.ds(t, 1), :].rearrange("p a d -> p (a d)"),
                                                  mv2[:, bass.ds(t, 1), 0:1].rearrange("p a d -> p (a d)"),
                                                  rstd2[:, bass.ds(t, 1)], ALU.subtract, ALU.mult)
                ins.then_inc(xn2_ready, 1)

            def x2_trailing(i, o):
                dve.wait_ge(x2_hi_ready, i * 2 + (o + 1))
                nc.vector.tensor_tensor(x2_lo[:, o % 2, :], psum[:, prep_bank(i, o, 6), :], x2_hi[:, o % 2, :].bitcast(F32), ALU.subtract).then_inc(x2_lo_ready, 1)

            def route(i, o, k):
                j = i * 2 + o
                if k > 0:
                    dve.wait_ge(route_step, j * ROUTE + k)
                    dve.sem_inc(passed, 1)
                r, part = divmod(k - 5, 6)

                def over_e(t):
                    return t[:].unsqueeze(2).broadcast_to([P, GB, E])

                if k == 0:
                    dve.wait_ge(lg_done, j + 1)
                    dve.sem_inc(passed, 1)
                    ins = nc.vector.tensor_tensor(logits[:], psum[:, prep_bank(i, o, 7), 0:GB * E].rearrange("p (b e) -> p b e", b=GB),
                                                  gb_bc[:].unsqueeze(1).broadcast_to([P, GB, E]), ALU.add)
                elif k == 1:
                    ins = nc.vector.tensor_reduce(top[:], logits[:], AX.X, ALU.max)
                elif k == 2:
                    ins = nc.vector.tensor_tensor(logits[:], logits[:], over_e(top), ALU.subtract)
                elif k == 3:
                    dve.wait_ge(soft_exp, j + 1)
                    dve.sem_inc(passed, 1)
                    ins = nc.vector.tensor_reduce(total[:], weights[:], AX.X, ALU.add)
                elif k == 4:
                    ins = nc.vector.reciprocal(inverse[:], total[:])
                elif k == ROUTE - 4:
                    ins = nc.vector.scalar_tensor_tensor(pick[:], left[:], -0.5, weights[:], ALU.is_lt, ALU.mult)
                elif k == ROUTE - 3:
                    ins = nc.vector.tensor_tensor(gates_f[:], pick[:], over_e(inverse), ALU.mult)
                elif k == ROUTE - 2:
                    if not isinstance(j, int) or j >= 2:
                        dve.wait_ge(gT_done, j - 1)
                        dve.sem_inc(passed, 1)
                    ins = nc.vector.tensor_copy(gate_cols[:, o % 2, :, 0:E], gates_f[:])
                elif k == ROUTE - 1:
                    ins = nc.vector.tensor_tensor(gate_cols[:, o % 2, :, 32:32 + E], gates_f[:],
                                                  gate_cols[:, o % 2, :, 0:E].bitcast(F32), ALU.subtract)
                elif part == 0:
                    ins = nc.vector.tensor_reduce(top[:], (left if r else weights)[:], AX.X, ALU.max)
                elif part == 1:
                    ins = nc.vector.tensor_tensor(pick[:], (left if r else weights)[:], over_e(top), ALU.is_equal)
                elif part == 2:
                    ins = nc.vector.tensor_tensor(pick[:], pick[:], rev_sb[:].unsqueeze(1).broadcast_to([P, GB, E]), ALU.mult)
                elif part == 3:
                    ins = nc.vector.tensor_reduce(place[:], pick[:], AX.X, ALU.max)
                elif part == 4:
                    ins = nc.vector.tensor_tensor(pick2[:], pick[:], over_e(place), ALU.is_equal)
                else:
                    ins = nc.vector.scalar_tensor_tensor(left[:], pick2[:], -2.0, (left if r else weights)[:], ALU.mult, ALU.add)
                ins.then_inc(route_step, 1)

            def slot(i, o):
                coming = below(i, o, B - GB)
                parts = PARTS[o % GB] if coming else ((), (), ())
                ended = o >= 2 and below(i, o, B + 2)
                if below(i, o + 1, B):
                    maxima(i, o + 1, 0)
                    maxima(i, o + 1, 1)
                if o >= 3:
                    residual(i, o - 3)
                if ended:
                    invert(i, o - 2)
                if o >= 3:
                    residual_stats(i, o - 3)
                if ended:
                    normalise(i, o - 2)
                if below(i, o + 1, B):
                    maxima(i, o + 1, 2)
                    maxima(i, o + 1, 3)
                for unit in parts[0]:
                    trailing(i, o // GB + 1, unit)
                if coming and o % GB == 0:
                    ln1_apply(i, o // GB + 1)
                if coming and o % GB == 1:
                    front_copy(i, o // GB + 1, 1)
                for unit in parts[1] + parts[2]:
                    trailing(i, o // GB + 1, unit)
                if coming and o % GB == 3:
                    front_copy(i, o // GB + 1, 3)
                if o % GB == 3 and below(i, o, B - 2 * GB):
                    ln1_stats(i, o // GB + 2)
                if not below(i, o, B - 2):
                    first = i * BODY + o - (B - 2)
                    if first == 0:
                        split_small()
                        ln2_stats(0, 0, GB)
                    elif first == 1:
                        normalise_group(0, 0)
                        ln2_stats(1, GB, B - GB)
                    elif first == 2:
                        x2_trailing(0, 0)
                    elif first == 3:
                        for k in range(3):
                            route(0, 0, k)
                    elif first == 4:
                        ln2_stats(2, B - GB, B)

            walk(dve, slot)
            def gate_hidden(i, o, c):
                j = i * 2 + o
                e = (c - CS) // CR
                dve.wait_ge(gelu_done, j * NCH + (c + 1))
                if (c - CS) % CR == 0:
                    dve.wait_ge(spread_done, j * E + (e + 1))
                dve.wait_ge(h_lo_ready, j * NCH + (c - 3))
                nc.vector.tensor_tensor(hid_gated[(2 * o + c) % 4], hid[:, c % 2, :], psum[:, 2 + e % 2, :], ALU.mult).then_inc(h_gated, 1)

            def trailing_h(i, o, c):
                m = (i * 2 + o) * NCH + c
                q = (2 * o + c) % 4
                dve.wait_ge(h_hi_ready, m + 1)
                if not isinstance(m, int) or m >= 4:
                    dve.wait_ge(l2_done, m - 3)
                nc.vector.tensor_tensor(h_lo[:, q, :], hid_gated[q], h_hi[:, q, :].bitcast(F32), ALU.subtract).then_inc(h_lo_ready, 1)

            def yT_leaves(i, o):
                j = i * 2 + o
                dve.wait_ge(l2_done, (j + 1) * NCH)
                nc.vector.tensor_copy(yT_sb, psum[:, 4 + o % 2, :]).then_inc(yT_out, 1)

            def result(i, o):
                j = i * 2 + o
                dve.wait_ge(y_turned, j + 1)
                dve.sem_inc(passed, 1)
                dve.wait_ge(out_free, j + 1)
                dve.sem_inc(passed, 1)
                nc.vector.scalar_tensor_tensor(out_buf[:, o % 2, :], psum[:, 6, :], tanh_g[:, 1:2],
                                               x_all[:, bass.ds(j * GB, GB), :].rearrange("p a d -> p (a d)"),
                                               ALU.mult, ALU.add).then_inc(y_ready, 1)

            def group(i, o):
                first = isinstance(i, int) and i * 2 + o == 0
                last = isinstance(i, int) and i * 2 + o == NG - 1
                for c in range(NCH):
                    if CS <= c + 1 < NCH:
                        gate_hidden(i, o, c + 1)
                    if not last:
                        if c == 0:
                            normalise_group(i, o + 1)
                        if c == 4:
                            x2_trailing(i, o + 1)
                        if 9 <= c <= 10:
                            route(i, o + 1, 2 * (c - 9))
                        if 18 <= c < 18 + (ROUTE - 3) // 2:
                            route(i, o + 1, 3 + 2 * (c - 18))
                    trailing_h(i, o, c)
                    if c == 2 and not first:
                        yT_leaves(i, o - 1)
                    if c == 14 and not first:
                        result(i, o - 1)
                    if not last:
                        if c == 9:
                            route(i, o + 1, 1)
                        if 18 <= c < 18 + (ROUTE - 3) // 2:
                            route(i, o + 1, 4 + 2 * (c - 18))
                    if first and c < 3:
                        for k in range(10 + 6 * c, min(16 + 6 * c, ROUTE)):
                            route(i, o, k)
                if last:
                    yT_leaves(i, o)
                    result(i, o)

            dve.wait_ge(gates_fill, 3)
            for k in range(3, 10):
                route(0, 0, k)
            walk_groups(dve, group)

        @block.tensor
        def _(pe):
            def front(i, gi, j):
                g = i * 2 + gi
                u = gi % 2
                ps = front_bank(g, j)
                later = not isinstance(g, int) or g > 0
                if j == 0 and later:
                    pe.wait_ge(v_out, g)
                if j == 1 and later or j == 3:
                    pe.wait_ge(parts_out, (g * 2 + (2 if j == 3 and later else 1)) * HG)
                if j == 1:
                    pe.wait_ge(xn_ready, g + 1)
                    for b in range(GB):
                        ins = nc.tensor.transpose(ps[:, b * S:(b + 1) * S], xn[:, b, :], ident_sb[:])
                elif j == 0:
                    pe.wait_ge(x_in, (g + 1) * 32)
                    ins = nc.tensor.matmul(ps[:, 0:GB * KP], w_kT[:], ctx_buf[:, u, :], start=True, stop=True)
                elif j == 2:
                    pe.wait_ge(xT_out, g + 1)
                    ins = nc.tensor.matmul(ps, w_qT[:], xnT[:], start=True, stop=True)
                else:
                    for b in range(GB):
                        ins = nc.tensor.matmul(ps[0:KV, b * P:(b + 1) * P], ctx_buf[:, u, b * KP:b * KP + KV], w_vT[:],
                                               start=True, stop=True)
                ins.then_inc(front_done, 1)

            def scores(i, o, g):
                n = i * BODY + o
                u, b = o // GB % 2, o % GB
                if b == 0 and g == 0:
                    pe.wait_ge(k_heads_ready, i * 2 + (o // GB + 1))
                if b == 0:
                    pe.wait_ge(parts_out, ((i * 2 + o // GB) * 2 + 1) * HG + (g + 1))
                if o >= 1 or g >= 2:
                    pe.wait_ge(max_done, n * 4 + (g - 1))
                rhs = k_heads[0:KS, u, g, :, b * KP:(b + 1) * KP]
                nc.tensor.matmul(s_ps[g % 2][:, 0:HQ * KP].rearrange("q (h k) -> q h k", h=HQ),
                                 q_stack[0:KS, u, g, b * S:(b + 1) * S], rhs, start=True, stop=True).then_inc(s_done, 1)

            def turn_max(i, o):
                n = i * BODY + o
                pe.wait_ge(max_done, n * 4 + 4)
                if o >= 4:
                    pe.wait_ge(x1_done, n - 3)
                nc.tensor.matmul(m_ps[:, 0:S], max_cols[:, o % 2, :], ident_r[:], start=True, stop=True).then_inc(mT_done, 1)

            def scores_t(i, o, g):
                n = i * BODY + o
                u, b = o // GB % 2, o % GB
                if g == 0:
                    pe.wait_ge(m_ready, n + 1)
                if o >= 1 or g >= 2:
                    pe.wait_ge(exp_done, n * 4 + (g - 1))
                for hh in range(HQ):
                    ins = nc.tensor.matmul(st_ps[g % 2][0:KV, hh * S:(hh + 1) * S], k_heads[:, u, g, hh, b * KP:b * KP + KV],
                                           q_stack[:, u, g, b * S:(b + 1) * S], start=True, stop=True)
                ins.then_inc(st_done, 1)

            def values(i, o, p, heads):
                n = i * BODY + o
                if p == 0 and heads[0] == 0:
                    pe.wait_ge(exp_done, n * 4 + 4)
                    pe.wait_ge(v_den_ready, n + 1)
                    if o >= 2:
                        pe.wait_ge(on_ready, n - 1)
                for h in heads:
                    ins = nc.tensor.matmul(o_ps[o % 2][p], v_den[:, o % 2, p, h * P:(h + 1) * P],
                                           probs[:, o % 2, (p * HH + h) * S:(p * HH + h + 1) * S],
                                           start=(h == 0), stop=(h == HH - 1))
                if heads[-1] == HH - 1:
                    ins.then_inc(av_done, 1)

            def project(i, o):
                n = i * BODY + o
                pe.wait_ge(on_ready, n + 1)
                if below(i, o + 3, B):
                    pe.wait_ge(m_ready, n + 4)
                else:
                    pe.wait_ge(x1_done, n)
                nc.tensor.matmul(y_ps, onT[:, o % 2, :], w_oT[:], start=True, stop=True).then_inc(wo_done, 1)

            pe.wait_ge(w_in, 6 * 16)
            for j in range(NF):
                front(0, 0, j)
            pe.wait_ge(k_half_ready, 1)
            for g in range(HG):
                scores(0, 0, g)

            def turn_x2(i, o):
                j = i * 2 + o
                pe.wait_ge(xn2_ready, j + 1)
                for b in range(GB):
                    ins = nc.tensor.transpose(psum[:, prep_bank(i, o, 6), b * S:(b + 1) * S], xn[:, b, :], ident_sb[:])
                ins.then_inc(x2T_done, 1)

            def logits_turned(i, o):
                j = i * 2 + o
                pe.wait_ge(x2_lo_ready, j + 1)
                if not isinstance(j, int) or j > 0:
                    pe.wait_ge(gT_out, j)
                ps = psum[0:E, prep_bank(i, o, 7), :]
                nc.tensor.matmul(ps, gw_parts[:, 0, :], x2_hi[:, o % 2, :], start=True, stop=False)
                nc.tensor.matmul(ps, gw_parts[:, 0, :], x2_lo[:, o % 2, :], start=False, stop=False)
                nc.tensor.matmul(ps, gw_parts[:, 1, :], x2_hi[:, o % 2, :], start=False, stop=True).then_inc(lgT_done, 1)

            def turn_logits(i, o):
                pe.wait_ge(lgT_out, i * 2 + (o + 1))
                pe.sem_inc(passed, 1)
                for b in range(GB):
                    ins = nc.tensor.transpose(psum[:, prep_bank(i, o, 7), b * E:(b + 1) * E], lgT[:, b * S:(b + 1) * S], ident_sb[0:E, 0:E])
                ins.then_inc(lg_done, 1)

            def layer1(i, o, c):
                j = i * 2 + o
                m = j * NCH + c
                if not isinstance(m, int) or m >= 2:
                    pe.wait_ge(gelu_done, m - 1)
                if isinstance(j, int) and j == 0 and c % 2 == 0:
                    pe.wait_ge(w_split, c + 2)
                ps = psum[:, c % 2, :]
                nc.tensor.matmul(ps, w_hi[:, 0, c, :], x2_hi[:, o % 2, :], start=True, stop=False)
                nc.tensor.matmul(ps, w_hi[:, 0, c, :], x2_lo[:, o % 2, :], start=False, stop=False)
                nc.tensor.matmul(ps, w_lo[:, 0, c, :], x2_hi[:, o % 2, :], start=False, stop=True).then_inc(l1_done, 1)

            def slot(i, o):
                pieces = PIECES[o % GB] if below(i, o, B - GB) else (None, None, None)
                now, ahead, behind = below(i, o, B), below(i, o + 1, B), o >= 1 and below(i, o, B + 1)
                early, late = range(HH // 2), range(HH // 2, HH)
                if now:
                    scores_t(i, o, 0)
                    scores_t(i, o, 1)
                if ahead:
                    scores(i, o + 1, 0)
                    scores(i, o + 1, 1)
                if o >= 3:
                    project(i, o - 3)
                if pieces[0] is not None:
                    front(i, o // GB + 1, pieces[0])
                if behind:
                    values(i, o - 1, 0, early)
                if ahead:
                    scores(i, o + 1, 2)
                    scores(i, o + 1, 3)
                if behind:
                    values(i, o - 1, 0, late)
                if now:
                    scores_t(i, o, 2)
                    scores_t(i, o, 3)
                if pieces[1] is not None:
                    front(i, o // GB + 1, pieces[1])
                if behind:
                    values(i, o - 1, 1, early)
                if ahead:
                    turn_max(i, o + 1)
                if pieces[2] is not None:
                    front(i, o // GB + 1, pieces[2])
                if behind:
                    values(i, o - 1, 1, late)
                if not below(i, o, B - 1):
                    if i * BODY + o == B - 1:
                        turn_x2(0, 0)
                    elif i * BODY + o == B:
                        pe.wait_ge(b2_split, 4)
                        logits_turned(0, 0)
                        for c in range(2):
                            layer1(0, 0, c)
                    elif i * BODY + o == B + 1:
                        turn_logits(0, 0)

            pe.wait_ge(id_ready, 1)
            turn_max(0, 0)
            walk(pe, slot)
            def turn_gates(i, o):
                pe.wait_ge(route_step, (i * 2 + (o + 1)) * ROUTE)
                for b in range(GB):
                    ins = nc.tensor.matmul(psum[0:32 + E + 1, prep_bank(i, o, 7), b * S:(b + 1) * S], gate_cols[:, o % 2, b, :], ident_r[:],
                                           start=True, stop=True)
                ins.then_inc(gT_done, 1)

            def spread_gates(i, o, e):
                j = i * 2 + o
                if e == 0:
                    pe.wait_ge(gT_out, j + 1)
                before = j * (NCH - CS) + (e - 1) * CR
                if not isinstance(before, int) or before > 0:
                    pe.wait_ge(h_gated, before)
                nc.tensor.matmul(psum[:, 2 + e % 2, :], gate_pick_r[:, e:e + 1].broadcast_to([P, P]), gatesT[:, o % 2, :],
                                 start=True, stop=True).then_inc(spread_done, 1)

            def layer2(i, o, c):
                m = (i * 2 + o) * NCH + c
                q = (2 * o + c) % 4
                pe.wait_ge(h_hi_ready, m + 1)
                pe.wait_ge(h_lo_ready, m + 1)
                ps = psum[:, 4 + o % 2, :]
                nc.tensor.matmul(ps, w_hi[:, 1, c, :], h_hi[:, q, :], start=False, stop=False, skip_group_check=True)
                nc.tensor.matmul(ps, w_hi[:, 1, c, :], h_lo[:, q, :], start=False, stop=False, skip_group_check=True)
                nc.tensor.matmul(ps, w_lo[:, 1, c, :], h_hi[:, q, :], start=False, stop=c == NCH - 1, skip_group_check=True).then_inc(l2_done, 1)

            def start_yT(i, o):
                j = i * 2 + o
                for k, part in enumerate((x2_hi, x2_lo)):
                    nc.tensor.matmul(psum[:, 4 + o % 2, :], ident_r[:], part[:, o % 2, :], start=k == 0, stop=False, skip_group_check=True)

            def output_biases(i, o):
                pe.wait_ge(gT_out, i * 2 + (o + 1))
                for part in range(2):
                    nc.tensor.matmul(psum[:, 4 + o % 2, :], b2_parts[:, part, :], gatesT[:, o % 2, :], start=False, stop=False, skip_group_check=True)

            def turn_yT(i, o):
                j = i * 2 + o
                pe.wait_ge(yT_out, j + 1)
                if not isinstance(j, int) or j < NG - 2:
                    pe.wait_ge(x2_lo_ready, j + 3)
                elif j == NG - 1:
                    pe.wait_ge(y_ready, j)
                for b in range(GB):
                    ins = nc.tensor.transpose(psum[:, 6, b * S:(b + 1) * S], yT_sb[:, b * S:(b + 1) * S], ident_sb[:])
                ins.then_inc(y_turned, 1)

            def group(i, o):
                first = isinstance(i, int) and i * 2 + o == 0
                last = isinstance(i, int) and i * 2 + o == NG - 1
                for c in range(NCH):
                    ahead = c + AHEAD
                    if ahead < NCH:
                        layer1(i, o, ahead)
                    elif not last:
                        layer1(i, o + 1, ahead - NCH)
                    if c == 0:
                        start_yT(i, o)
                    layer2(i, o, c)
                    if first and c == 1:
                        turn_gates(0, 0)
                    if CS <= ahead < NCH and (ahead - CS) % CR == 0:
                        spread_gates(i, o, (ahead - CS) // CR)
                    if c == 2:
                        output_biases(i, o)
                    if c == 9 and not first:
                        turn_yT(i, o - 1)
                    if not last:
                        if c == 0:
                            turn_x2(i, o + 1)
                        if c == 4:
                            logits_turned(i, o + 1)
                        if c == 6:
                            turn_logits(i, o + 1)
                        if c == 30:
                            turn_gates(i, o + 1)
                if last:
                    turn_yT(i, o)

            layer1(0, 0, 2)
            pe.wait_ge(x1_done, B)
            walk_groups(pe, group)


_INS = ["x", "ctxT", "g_xattn", "g_ffn", "wqT", "wkT", "wvT", "woT", "w_chunks", "b1_cols", "b2",
        "gW", "gb", "ident", "head_of_row", "gate_rows", "rev_idx"]


def kernel(**inputs):
    import numpy as np
    import concourse.bacc as bacc
    from concourse.bass_utils import run_bass_kernel_spmd

    data = {k.replace("L0_xattn_", "").replace("L0_ffn_", ""): np.asarray(v) for k, v in inputs.items()}
    ctx = data.pop("ctx_1024")
    ctx = np.concatenate([ctx, ctx[:, -1:]], axis=1)
    data["ctxT"] = ctx.transpose(2, 0, 1).reshape(ctx.shape[2], -1)
    for n in "qkvo":
        data[f"w{n}T"] = data.pop(f"w_{n}").T
    d = data["sW1"].shape[1]
    w1 = np.concatenate([w.reshape(len(w), d, -1, P).transpose(1, 0, 2, 3).reshape(d, -1, P) for w in (data["sW1"], data["rW1"])], axis=1)
    w2 = np.concatenate([w.reshape(-1, P, d).transpose(1, 0, 2) for w in (data["sW2"], data["rW2"])], axis=1)
    data["w_chunks"] = np.stack([w1, w2], axis=1)
    data["b1_cols"] = np.concatenate([b.reshape(-1, P) for b in (data["sb1"], data["rb1"])]).T
    data["b2"] = np.concatenate([data["rb2"], data["sb2"]])
    rows = np.arange(P)
    heads = np.where(rows < 96, rows // 8 % 4, rows - 96)
    data["ident"] = np.eye(P, dtype=np.float32)
    data["head_of_row"] = (heads[:, None] == np.arange(4)[None]).astype(np.float32)
    experts = data["gW"].shape[1]
    data["gate_rows"] = (rows[:, None] % 32 == np.arange(16)[None]).astype(np.float32) * (rows[:, None] < 64)
    data["gate_rows"] = data["gate_rows"].astype(np.float32)
    data["rev_idx"] = np.broadcast_to(experts - np.arange(experts, dtype=np.float32), (P, experts))

    nc = bacc.Bacc("TRN2", target_bir_lowering=False, num_devices=1)
    arrays, args = {}, []
    for name in _INS:
        a = np.ascontiguousarray(data[name])
        arrays[f"in_{name}"] = a
        args.append(nc.dram_tensor(f"in_{name}", a.shape, mybir.dt.from_np(a.dtype), kind="ExternalInput").ap())
    shape = data["x"].shape
    args.append(nc.dram_tensor("out_0", shape, F32, kind="ExternalOutput").ap())
    flamingo_kernel(nc, *args)
    r = run_bass_kernel_spmd(nc, [arrays], core_ids=[0])
    return r.results[0]["out_0"]
```
